# Optimizing a Trainium2 kernel written in Bass

```python
import numpy as np
import jax
import jax.numpy as jnp

def _softmax(x, axis=-1):
    return jax.nn.softmax(x, axis=axis)

def _gelu(x):
    return jax.nn.gelu(x, approximate=True)

def _silu(x):
    return jax.nn.silu(x)

def _sigmoid(x):
    return jax.nn.sigmoid(x)

def _layernorm(x, axis=-1, eps=1e-05):
    m = jnp.mean(x, axis=axis, keepdims=True)
    v = jnp.var(x, axis=axis, keepdims=True)
    return (x - m) / jnp.sqrt(v + eps)

def _scatter_add(tgt, idx, src, axis=0):
    return tgt.at[idx].add(src)

def _segment_sum(src, seg, n):
    return jax.ops.segment_sum(src, seg, n)
kernel_name = 'mk_prb_d2_jaxref_r8_5d7f11'

def setup_inputs(seed: int=0):
    np.random.seed(seed)
    _w = jnp.asarray

    def _L0_attn_setup():
        import jax, jax.numpy as jnp
        import numpy as np
        B, T, D, H = (2, 256, 256, 16)
        DH = D // H
        ROPE_BASE = 10000.0

        def _rope(x, cos, sin):
            x0 = x[..., 0::2]
            x1 = x[..., 1::2]
            r0 = cos * x0 - sin * x1
            r1 = sin * x0 + cos * x1
            return jnp.stack((r0, r1), axis=-1).reshape(x.shape)
        key = jax.random.key(seed)
        ks = jax.random.split(key, 5)
        s = D ** (-0.5)
        return {'X': jax.random.normal(ks[0], (B, T, D), dtype=jnp.float32), 'Wq': jax.random.normal(ks[1], (D, D), dtype=jnp.float32) * s, 'Wk': jax.random.normal(ks[2], (D, D), dtype=jnp.float32) * s, 'Wv': jax.random.normal(ks[3], (D, D), dtype=jnp.float32) * s, 'Wo': jax.random.normal(ks[4], (D, D), dtype=jnp.float32) * s}
    _L0_attn_in = _L0_attn_setup()

    def _L0_ffn_setup():
        import jax, jax.numpy as jnp
        import numpy as np

        @jax.custom_vjp
        def ste_sign(x):
            return jnp.sign(x)

        def _ste_fwd(x):
            return (jnp.sign(x), None)

        def _ste_bwd(_, g):
            return (g,)
        ste_sign.defvjp(_ste_fwd, _ste_bwd)
        D_MODEL = 256
        D_HIDDEN = 1024
        key = jax.random.key(seed)
        k_x, k_up, k_dn = jax.random.split(key, 3)
        x = jax.random.normal(k_x, (2, 256, D_MODEL), dtype=jnp.float32)
        up_weight = jax.random.normal(k_up, (D_HIDDEN, D_MODEL), dtype=jnp.float32) * 0.02
        down_weight = jax.random.normal(k_dn, (D_MODEL, D_HIDDEN), dtype=jnp.float32) * 0.02
        up_scale = jnp.ones((D_HIDDEN,), dtype=jnp.float32)
        down_scale = jnp.ones((D_MODEL,), dtype=jnp.float32)
        output_scale = jnp.ones((1,), dtype=jnp.float32)
        return {'x': x, 'up_weight': up_weight, 'down_weight': down_weight, 'up_scale': up_scale, 'down_scale': down_scale, 'output_scale': output_scale}
    _L0_ffn_in = _L0_ffn_setup()

    def _L1_attn_setup():
        import jax, jax.numpy as jnp
        import numpy as np
        B, S, D_MODEL = (2, 256, 256)
        H, DS, DG, DV = (16, 64, 64, 128)
        ROPE_BASE = 10000.0
        NEG_INF = -1000000000.0

        def _rope(x, base=ROPE_BASE):
            d = x.shape[-1]
            half = d // 2
            inv_freq = 1.0 / base ** (jnp.arange(half, dtype=jnp.float32) / half)
            ang = jnp.arange(x.shape[1], dtype=jnp.float32)[:, None] * inv_freq
            cos = jnp.cos(ang)[None, :, None, :]
            sin = jnp.sin(ang)[None, :, None, :]
            x1, x2 = (x[..., :half], x[..., half:])
            return jnp.concatenate([x1 * cos - x2 * sin, x1 * sin + x2 * cos], axis=-1)
        key = jax.random.key(seed)
        ks = jax.random.split(key, 8)
        s = lambda fan_in: 1.0 / np.sqrt(fan_in)
        return {'x': jax.random.normal(ks[0], (B, S, D_MODEL), dtype=jnp.float32), 'wq_sem': jax.random.normal(ks[1], (D_MODEL, H * DS), dtype=jnp.float32) * s(D_MODEL), 'wk_sem': jax.random.normal(ks[2], (D_MODEL, H * DS), dtype=jnp.float32) * s(D_MODEL), 'wq_geo': jax.random.normal(ks[3], (D_MODEL, H * DG), dtype=jnp.float32) * s(D_MODEL), 'wk_geo': jax.random.normal(ks[4], (D_MODEL, H * DG), dtype=jnp.float32) * s(D_MODEL), 'wv': jax.random.normal(ks[5], (D_MODEL, H * DV), dtype=jnp.float32) * s(D_MODEL), 'wo': jax.random.normal(ks[6], (H * DV, D_MODEL), dtype=jnp.float32) * s(H * DV), 'gate_logit': jax.random.normal(ks[7], (H,), dtype=jnp.float32)}
    _L1_attn_in = _L1_attn_setup()

    def _L1_ffn_setup():
        import jax, jax.numpy as jnp
        import numpy as np
        HIDDEN = 256
        NUM_EXPERTS = 32
        TOP_K = 4
        D_MOE = 96
        D_SHARED = 512
        B, S = (1, 256)

        def _moe_forward(hidden_states, gate_w, gate_up_proj, down_proj, shared_gate_w, shared_up_w, shared_down_w, shared_expert_gate_w):
            Bb, Ss, d = hidden_states.shape
            x = hidden_states.reshape(-1, d)
            T = x.shape[0]
            router_logits = x @ gate_w.T
            routing_weights = jax.nn.softmax(router_logits.astype(jnp.float32), axis=-1)
            topk_w, topk_idx = jax.lax.top_k(routing_weights, TOP_K)
            topk_w = topk_w / (jnp.sum(topk_w, axis=-1, keepdims=True) + 1e-20)
            topk_w = topk_w.astype(x.dtype)
            comb = jnp.zeros((T, NUM_EXPERTS), x.dtype).at[jnp.arange(T)[:, None], topk_idx].add(topk_w)
            sh = jax.nn.silu(x @ shared_gate_w.T) * (x @ shared_up_w.T)
            shared_out = sh @ shared_down_w.T
            shared_gate = jax.nn.sigmoid(x @ shared_expert_gate_w.T)
            out0 = shared_gate * shared_out

            def body(acc, inp):
                gu_w, dn_w, w_e = inp
                gu = x @ gu_w.T
                gate, up = (gu[:, :D_MOE], gu[:, D_MOE:])
                h = jax.nn.silu(gate) * up
                y = h @ dn_w.T
                return (acc + w_e[:, None] * y, None)
            out, _ = jax.lax.scan(body, out0, (gate_up_proj, down_proj, comb.T))
            return out.reshape(Bb, Ss, d)
        key = jax.random.key(seed)
        ks = jax.random.split(key, 8)
        sc = 0.02
        return {'hidden_states': jax.random.normal(ks[0], (B, S, HIDDEN), jnp.float32), 'gate_w': jax.random.normal(ks[1], (NUM_EXPERTS, HIDDEN), jnp.float32) * sc, 'gate_up_proj': jax.random.normal(ks[2], (NUM_EXPERTS, 2 * D_MOE, HIDDEN), jnp.float32) * sc, 'down_proj': jax.random.normal(ks[3], (NUM_EXPERTS, HIDDEN, D_MOE), jnp.float32) * sc, 'shared_gate_w': jax.random.normal(ks[4], (D_SHARED, HIDDEN), jnp.float32) * sc, 'shared_up_w': jax.random.normal(ks[5], (D_SHARED, HIDDEN), jnp.float32) * sc, 'shared_down_w': jax.random.normal(ks[6], (HIDDEN, D_SHARED), jnp.float32) * sc, 'shared_expert_gate_w': jax.random.normal(ks[7], (1, HIDDEN), jnp.float32) * sc}
    _L1_ffn_in = _L1_ffn_setup()
    _d = {'L0_attn_X': _L0_attn_in['X'], 'L0_attn_Wq': _L0_attn_in['Wq'], 'L0_attn_Wk': _L0_attn_in['Wk'], 'L0_attn_Wv': _L0_attn_in['Wv'], 'L0_attn_Wo': _L0_attn_in['Wo'], 'L0_ffn_up_weight': _L0_ffn_in['up_weight'], 'L0_ffn_down_weight': _L0_ffn_in['down_weight'], 'L0_ffn_up_scale': _L0_ffn_in['up_scale'], 'L0_ffn_down_scale': _L0_ffn_in['down_scale'], 'L0_ffn_output_scale': _L0_ffn_in['output_scale'], 'L1_attn_wq_sem': _L1_attn_in['wq_sem'], 'L1_attn_wk_sem': _L1_attn_in['wk_sem'], 'L1_attn_wq_geo': _L1_attn_in['wq_geo'], 'L1_attn_wk_geo': _L1_attn_in['wk_geo'], 'L1_attn_wv': _L1_attn_in['wv'], 'L1_attn_wo': _L1_attn_in['wo'], 'L1_attn_gate_logit': _L1_attn_in['gate_logit'], 'L1_ffn_gate_w': _L1_ffn_in['gate_w'], 'L1_ffn_gate_up_proj': _L1_ffn_in['gate_up_proj'], 'L1_ffn_down_proj': _L1_ffn_in['down_proj'], 'L1_ffn_shared_gate_w': _L1_ffn_in['shared_gate_w'], 'L1_ffn_shared_up_w': _L1_ffn_in['shared_up_w'], 'L1_ffn_shared_down_w': _L1_ffn_in['shared_down_w'], 'L1_ffn_shared_expert_gate_w': _L1_ffn_in['shared_expert_gate_w']}
    _x0 = _d['L0_attn_X']
    _d['L0_attn_X'] = jax.random.normal(jax.random.fold_in(jax.random.key(seed), 1), (1, 1024, 256), dtype=_x0.dtype)
    del _x0
    return _d

def reference(L0_attn_X, L0_attn_Wq, L0_attn_Wk, L0_attn_Wv, L0_attn_Wo, L0_ffn_up_weight, L0_ffn_down_weight, L0_ffn_up_scale, L0_ffn_down_scale, L0_ffn_output_scale, L1_attn_wq_sem, L1_attn_wk_sem, L1_attn_wq_geo, L1_attn_wk_geo, L1_attn_wv, L1_attn_wo, L1_attn_gate_logit, L1_ffn_gate_w, L1_ffn_gate_up_proj, L1_ffn_down_proj, L1_ffn_shared_gate_w, L1_ffn_shared_up_w, L1_ffn_shared_down_w, L1_ffn_shared_expert_gate_w):

    def _L0_attn_ref(X, Wq, Wk, Wv, Wo):
        import jax, jax.numpy as jnp
        import numpy as np
        B, T, D, H = (2, 256, 256, 16)
        DH = D // H
        ROPE_BASE = 10000.0

        def _rope(x, cos, sin):
            x0 = x[..., 0::2]
            x1 = x[..., 1::2]
            r0 = cos * x0 - sin * x1
            r1 = sin * x0 + cos * x1
            return jnp.stack((r0, r1), axis=-1).reshape(x.shape)
        b, t, d = X.shape
        Q = X @ Wq.T
        K = X @ Wk.T
        V = X @ Wv.T
        Qh = Q.reshape(b, t, H, DH).transpose(0, 2, 1, 3)
        Kh = K.reshape(b, t, H, DH).transpose(0, 2, 1, 3)
        Vh = V.reshape(b, t, H, DH).transpose(0, 2, 1, 3)
        theta = ROPE_BASE ** (-2.0 * jnp.arange(DH // 2, dtype=jnp.float32) / DH)
        angles = jnp.arange(t, dtype=jnp.float32)[:, None] * theta[None, :]
        cos = jnp.cos(angles).astype(X.dtype)
        sin = jnp.sin(angles).astype(X.dtype)
        Qr = _rope(Qh, cos, sin)
        Kr = _rope(Kh, cos, sin)
        scores = jnp.einsum('bhqd,bhkd->bhqk', Qr, Kr) * DH ** (-0.5)
        causal = jnp.triu(jnp.ones((t, t), dtype=bool), 1)
        scores = jnp.where(causal, jnp.finfo(scores.dtype).min, scores)
        pattern = jax.nn.softmax(scores, axis=-1)
        heads = jnp.einsum('bhqk,bhkd->bqhd', pattern, Vh).reshape(b, t, d)
        return heads @ Wo.T

    def _L0_ffn_ref(x, up_weight, down_weight, up_scale, down_scale, output_scale):
        import jax, jax.numpy as jnp
        import numpy as np

        @jax.custom_vjp
        def ste_sign(x):
            return jnp.sign(x)

        def _ste_fwd(x):
            return (jnp.sign(x), None)

        def _ste_bwd(_, g):
            return (g,)
        ste_sign.defvjp(_ste_fwd, _ste_bwd)
        D_MODEL = 256
        D_HIDDEN = 1024
        up_w = ste_sign(up_weight)
        down_w = ste_sign(down_weight)
        hidden = jnp.einsum('bsd,hd->bsh', x, up_w) * up_scale
        hidden = jax.nn.relu(hidden)
        out = jnp.einsum('bsh,dh->bsd', hidden, down_w) * down_scale
        return out * output_scale

    def _L1_attn_ref(x, wq_sem, wk_sem, wq_geo, wk_geo, wv, wo, gate_logit):
        import jax, jax.numpy as jnp
        import numpy as np
        B, S, D_MODEL = (2, 256, 256)
        H, DS, DG, DV = (16, 64, 64, 128)
        ROPE_BASE = 10000.0
        NEG_INF = -1000000000.0

        def _rope(x, base=ROPE_BASE):
            d = x.shape[-1]
            half = d // 2
            inv_freq = 1.0 / base ** (jnp.arange(half, dtype=jnp.float32) / half)
            ang = jnp.arange(x.shape[1], dtype=jnp.float32)[:, None] * inv_freq
            cos = jnp.cos(ang)[None, :, None, :]
            sin = jnp.sin(ang)[None, :, None, :]
            x1, x2 = (x[..., :half], x[..., half:])
            return jnp.concatenate([x1 * cos - x2 * sin, x1 * sin + x2 * cos], axis=-1)
        b, sl, _ = x.shape
        qs = (x @ wq_sem).reshape(b, sl, H, DS)
        ksem = (x @ wk_sem).reshape(b, sl, H, DS)
        qg = _rope((x @ wq_geo).reshape(b, sl, H, DG))
        kg = _rope((x @ wk_geo).reshape(b, sl, H, DG))
        v = (x @ wv).reshape(b, sl, H, DV)
        sem_scale = 1.0 / np.sqrt(DS)
        geo_scale = 1.0 / np.sqrt(DG)
        sem_scores = jnp.einsum('bqhd,bkhd->bhqk', qs, ksem) * sem_scale
        geo_scores = jnp.einsum('bqhd,bkhd->bhqk', qg, kg) * geo_scale
        g = jax.nn.sigmoid(gate_logit)[None, :, None, None]
        scores = g * sem_scores + (1.0 - g) * geo_scores
        causal = jnp.tril(jnp.ones((sl, sl), dtype=bool))
        scores = jnp.where(causal[None, None], scores, NEG_INF)
        attn = jax.nn.softmax(scores, axis=-1)
        out = jnp.einsum('bhqk,bkhd->bqhd', attn, v).reshape(b, sl, H * DV)
        return out @ wo

    def _L1_ffn_ref(hidden_states, gate_w, gate_up_proj, down_proj, shared_gate_w, shared_up_w, shared_down_w, shared_expert_gate_w):
        import jax, jax.numpy as jnp
        import numpy as np
        HIDDEN = 256
        NUM_EXPERTS = 32
        TOP_K = 4
        D_MOE = 96
        D_SHARED = 512
        B, S = (1, 256)

        def _moe_forward(hidden_states, gate_w, gate_up_proj, down_proj, shared_gate_w, shared_up_w, shared_down_w, shared_expert_gate_w):
            Bb, Ss, d = hidden_states.shape
            x = hidden_states.reshape(-1, d)
            T = x.shape[0]
            router_logits = x @ gate_w.T
            routing_weights = jax.nn.softmax(router_logits.astype(jnp.float32), axis=-1)
            topk_w, topk_idx = jax.lax.top_k(routing_weights, TOP_K)
            topk_w = topk_w / (jnp.sum(topk_w, axis=-1, keepdims=True) + 1e-20)
            topk_w = topk_w.astype(x.dtype)
            comb = jnp.zeros((T, NUM_EXPERTS), x.dtype).at[jnp.arange(T)[:, None], topk_idx].add(topk_w)
            sh = jax.nn.silu(x @ shared_gate_w.T) * (x @ shared_up_w.T)
            shared_out = sh @ shared_down_w.T
            shared_gate = jax.nn.sigmoid(x @ shared_expert_gate_w.T)
            out0 = shared_gate * shared_out

            def body(acc, inp):
                gu_w, dn_w, w_e = inp
                gu = x @ gu_w.T
                gate, up = (gu[:, :D_MOE], gu[:, D_MOE:])
                h = jax.nn.silu(gate) * up
                y = h @ dn_w.T
                return (acc + w_e[:, None] * y, None)
            out, _ = jax.lax.scan(body, out0, (gate_up_proj, down_proj, comb.T))
            return out.reshape(Bb, Ss, d)
        return _moe_forward(hidden_states, gate_w, gate_up_proj, down_proj, shared_gate_w, shared_up_w, shared_down_w, shared_expert_gate_w)
    x = L0_attn_X
    xn = _layernorm(x, axis=-1)
    x = x + _L0_attn_ref(xn, L0_attn_Wq, L0_attn_Wk, L0_attn_Wv, L0_attn_Wo) + _L0_ffn_ref(xn, L0_ffn_up_weight, L0_ffn_down_weight, L0_ffn_up_scale, L0_ffn_down_scale, L0_ffn_output_scale)
    xn = _layernorm(x, axis=-1)
    x = x + _L1_attn_ref(xn, L1_attn_wq_sem, L1_attn_wk_sem, L1_attn_wq_geo, L1_attn_wk_geo, L1_attn_wv, L1_attn_wo, L1_attn_gate_logit) + _L1_ffn_ref(xn, L1_ffn_gate_w, L1_ffn_gate_up_proj, L1_ffn_down_proj, L1_ffn_shared_gate_w, L1_ffn_shared_up_w, L1_ffn_shared_down_w, L1_ffn_shared_expert_gate_w)
    return x

_drawn_inputs = setup_inputs


def setup_inputs(seed=0):
    import zlib

    import numpy as np

    out = dict(_drawn_inputs(seed))
    spreads = {'L0_ffn_up_scale': (1.0, 0.2), 'L0_ffn_down_scale': (1.0, 0.2)}
    factors = {'L0_attn_Wq': 8.0,
     'L0_attn_Wk': 8.0,
     'L0_attn_Wv': 8.0,
     'L0_attn_Wo': 8.0,
     'L1_attn_wq_sem': 8.0,
     'L1_attn_wk_sem': 8.0,
     'L1_attn_wq_geo': 8.0,
     'L1_attn_wk_geo': 8.0,
     'L1_attn_wv': 8.0,
     'L1_attn_wo': 8.0,
     'L1_attn_gate_logit': 8.0,
     'L1_ffn_gate_w': 44.489,
     'L1_ffn_gate_up_proj': 42.836,
     'L1_ffn_down_proj': 42.825,
     'L1_ffn_shared_gate_w': 22.195,
     'L1_ffn_shared_up_w': 8.0,
     'L1_ffn_shared_down_w': 8.0,
     'L1_ffn_shared_expert_gate_w': 34.919}
    for name, (base, spread) in spreads.items():
        noise = np.random.default_rng([zlib.crc32(name.encode()), seed]).standard_normal(out[name].shape)
        drawn = base * np.exp(spread * noise) if base else spread * noise
        out[name] = jnp.asarray(drawn.astype(out[name].dtype))
    for name, factor in factors.items():
        out[name] = (out[name] * factor).astype(out[name].dtype)
    return out
```

```python
from contextlib import ExitStack

import concourse.bass as bass
from concourse import mybir

F32 = mybir.dt.float32
F32R = mybir.dt.float32r
BF16 = mybir.dt.bfloat16
U32 = mybir.dt.uint32
ALU = mybir.AluOpType
ACT = mybir.ActivationFunctionType
AX_X = mybir.AxisListType.X

P = 128
T = 1024
D = 256
KT = D // P
NT = T // P
CH = 512
NC = T // CH
TPC = CH // P
EPS = 1e-5

H0 = 16
DH0 = D // H0
HALF0 = DH0 // 2
GH = 4
NG = H0 // GH
HID = 1024
UT = HID // P
STACK = 4 * DH0

H1 = 16
DS = 64
DV = 128
NE = 32
TOPK = 4
DMOE = 96
EG = 4
ET = EG * DMOE // P
NEG = NE // EG
SH = 512
ST = SH // P
HPI = H1 // NEG
assert HPI == 2 and ET == 3

T_UNITS = [(i, j, min(4, i + 1 - j)) for i in range(NT) for j in range(0, i + 1, 4)]
NTU = len(T_UNITS)
TU_OF = [[n for n, u in enumerate(T_UNITS) if u[0] == i] for i in range(NT)]


def score_chunks(i):
    width = (i + 1) * P
    return [(c, min(CH, width - c)) for c in range(0, width, CH)]


def pv_pieces(c):
    return [(j, max(0, j * P - c * CH)) for j in range((c + 1) * TPC)]


def three(hi_hi, lo_hi, hi_lo):
    return (hi_hi, lo_hi, hi_lo)


class Semaphores:
    def __init__(self, nc, ctx, prefix):
        self.nc, self.ctx, self.prefix = nc, ctx, prefix

    def __call__(self, name):
        return self.ctx.enter_context(self.nc.semaphore(self.prefix + name))


def build(nc, d):
    with ExitStack() as ctx:
        def sb(name, shape, dt=F32, on=ctx):
            return on.enter_context(nc.sbuf_tensor(name, shape, dt))

        ident = sb("ident", [P, P])
        ident_bf = sb("ident_bf", [P, P], BF16)
        mask_bf = sb("mask_bf", [P, P], BF16)
        x = sb("x", [P, NT, D])
        xT_hi, xT_lo = sb("xT_hi", [P, KT, T], F32R), sb("xT_lo", [P, KT, T], F32R)
        acc = sb("acc", [P, KT, T])
        bank = ctx.enter_context(nc.psum_tensor("bank", [P, 8, CH], F32))
        rope_scratch = {
            n: nc.dram_tensor(f"{n}_stack", (H0, STACK, T), F32, kind="Internal").ap() for n in "qk"}
        comb_scratch = nc.dram_tensor("comb_scratch", (NE + 1, T), F32, kind="Internal").ap()

        with ExitStack() as layer0:
            v_sb = sb("v_sb", [P, NT, D], on=layer0)
            with ExitStack() as a:
                project_layer0(nc, d, a, sb, bank, x, acc, xT_hi, xT_lo, ident, ident_bf, mask_bf, v_sb, rope_scratch)
            heads_hi = sb("heads_hi", [P, NG, T], F32R, on=layer0)
            heads_lo = sb("heads_lo", [P, NG, T], F32R, on=layer0)
            with ExitStack() as b:
                attend_layer0(nc, d, b, sb, bank, ident, ident_bf, mask_bf, v_sb, rope_scratch,
                              heads_hi, heads_lo)
            with ExitStack() as c:
                join_layer0(nc, d, c, sb, bank, x, ident, heads_hi, heads_lo, xT_hi, xT_lo, acc,
                            comb_scratch)
        with ExitStack() as e:
            layer1(nc, d, e, sb, bank, ident, ident_bf, mask_bf, xT_hi, xT_lo, acc, comb_scratch)


class Norm:

    def __init__(self, nc, sb, on, prefix):
        self.nc = nc
        self.stats = sb(prefix + "stats", [P, NT, 6], on=on)
        self.mv = sb(prefix + "mv", [P, NT, 2], on=on)
        self.var = sb(prefix + "var", [P, NT], on=on)
        self.sd = sb(prefix + "sd", [P, NT], on=on)
        self.r0 = sb(prefix + "r0", [P, NT], on=on)
        self.r1 = sb(prefix + "r1", [P, NT], on=on)
        self.r2 = sb(prefix + "r2", [P, NT], on=on)
        self.r3 = sb(prefix + "r3", [P, NT], on=on)
        self.rstd = sb(prefix + "rstd", [P, NT], on=on)
        self.step = on.enter_context(nc.semaphore(prefix + "norm_step"))
        self.sqrt = on.enter_context(nc.semaphore(prefix + "norm_sqrt"))

    VAR_STEP = 2 * NT + 1

    def on_vector(self, dve, src, out):
        nc, n = self.nc, 0
        for j in range(NT):
            nc.vector.bn_stats(self.stats[:, j, :], src[:, j, :]).then_inc(self.step, 1)
        for j in range(NT):
            dve.wait_ge(self.step, NT)
            nc.vector.bn_aggr(self.mv[:, j, :], self.stats[:, j, :]).then_inc(self.step, 1)
        dve.wait_ge(self.step, 2 * NT)
        nc.vector.tensor_scalar(self.var[:], self.mv[:, :, 1], EPS, None, ALU.add).then_inc(self.step, 1)
        n = self.VAR_STEP
        dve.wait_ge(self.sqrt, 1)
        nc.vector.reciprocal(self.r0[:], self.sd[:]).then_inc(self.step, 1)
        dve.wait_ge(self.step, n + 1)
        nc.vector.tensor_tensor(self.r1[:], self.r0[:], self.r0[:], ALU.mult).then_inc(self.step, 1)
        dve.wait_ge(self.step, n + 2)
        nc.vector.tensor_tensor(self.r2[:], self.r1[:], self.var[:], ALU.mult).then_inc(self.step, 1)
        dve.wait_ge(self.step, n + 3)
        nc.vector.tensor_scalar(self.r3[:], self.r2[:], -0.5, 1.5, ALU.mult, ALU.add).then_inc(self.step, 1)
        dve.wait_ge(self.step, n + 4)
        nc.vector.tensor_tensor(self.rstd[:], self.r0[:], self.r3[:], ALU.mult).then_inc(self.step, 1)
        dve.wait_ge(self.step, n + 5)
        for j in range(NT):
            nc.vector.tensor_scalar(out[:, j, :], src[:, j, :], self.mv[:, j, 0:1], self.rstd[:, j:j + 1],
                                    ALU.subtract, ALU.mult).then_inc(self.step, 1)

    DONE = VAR_STEP + 5

    def on_scalar(self, act):
        act.wait_ge(self.step, self.VAR_STEP)
        self.nc.scalar.activation(self.sd[:], self.var[:], ACT.Sqrt).then_inc(self.sqrt, 1)


def project_layer0(nc, d, ctx, sb, bank, x, room, xT_hi, xT_lo, ident, ident_bf, mask_bf, v_sb, rope_scratch):
    sem = Semaphores(nc, ctx, "a_")

    def buf(name, shape, dt=F32):
        return sb("a_" + name, shape, dt, on=ctx)

    mask = buf("mask", [P, P])
    xn = room[:].rearrange("p k t -> p (k t)").rearrange("p (j d) -> p j d", j=NT)
    w = buf("w", [P, KT, 3 * D])
    w_hi, w_lo = buf("w_hi", [P, KT, 3 * D], F32R), buf("w_lo", [P, KT, 3 * D], F32R)
    table = {n: buf(n, [P, T]) for n in ("cos_q", "sin_q", "cos_k", "sin_k")}
    prod = [buf(f"prod{n}", [P, T]) for n in range(3)]
    rot = [buf(f"rot{n}", [P, T]) for n in range(1)]
    part_hi = [buf(f"part_hi{m}", [P, T], F32R) for m in range(4)]
    part_lo = [buf(f"part_lo{m}", [P, T], F32R) for m in range(4)]
    up = buf("up", [P, KT, HID])
    up_sign = buf("up_sign", [P, KT, HID], F32R)
    down = buf("down", [P, UT, D])
    down_sign = buf("down_sign", [P, UT, D], F32R)
    up_scale, down_scale, out_scale = buf("ups", [P, UT]), buf("downs", [P, D]), buf("outs", [P, 1])
    hid = [buf(f"hid{n}", [P, CH]) for n in range(2)]
    hid_hi, hid_lo = buf("hid_hi", [P, UT, CH], F32R), buf("hid_lo", [P, UT, CH], F32R)
    scaled = [buf(f"scaled{n}", [P, D]) for n in range(2)]
    norm = Norm(nc, sb, ctx, "a_")

    x_in, const_in, w_in, table_in, ffn_in = sem("x_in"), sem("const_in"), sem("w_in"), sem("table_in"), sem("ffn_in")
    consts = sem("consts")
    w_hi_done, w_lo_done, signs_done = sem("w_hi_done"), sem("w_lo_done"), sem("signs_done")
    transposed, xT_hi_done, xT_lo_done = sem("transposed"), sem("xT_hi_done"), sem("xT_lo_done")
    projected = sem("projected")
    rope_step = sem("rope_step")
    rot_hi_done = sem("rot_hi_done")
    v_projected, v_copied = sem("v_projected"), sem("v_copied")
    up_done, relu_done, hid_hi_done, hid_lo_done = sem("up_done"), sem("relu_done"), sem("hid_hi_done"), sem("hid_lo_done")
    down_done, down_scaled, x_added = sem("down_done"), sem("down_scaled"), sem("x_added")
    stored = sem("stored")

    STEPS = 4
    NU = NC * UT

    with nc.Block() as block:
        @block.sync
        def _(sp):
            sp.dma_start(x[:], d["x"].rearrange("(j p) d -> p j d", p=P)).then_inc(x_in, 16)
            sp.dma_start(ident[:], d["ident"]).then_inc(const_in, 16)
            sp.dma_start(mask[:], d["mask"]).then_inc(const_in, 16)
            sp.dma_start(w[:], d["w_qkv0"]).then_inc(w_in, 16)
            for n in table:
                sp.dma_start(table[n][:], d[n]).then_inc(table_in, 16)
            sp.dma_start(up[:], d["up0"]).then_inc(ffn_in, 16)
            sp.dma_start(down[:], d["down0"]).then_inc(ffn_in, 16)
            sp.dma_start(up_scale[:], d["up_scale"]).then_inc(ffn_in, 16)
            sp.dma_start(down_scale[:], d["down_scale"]).then_inc(ffn_in, 16)
            sp.dma_start(out_scale[:], d["out_scale"]).then_inc(ffn_in, 16)
            for m in range(4):
                which, half = "qk"[m // 2], m % 2
                sp.wait_ge(rope_step, STEPS * (m + 1))
                for rep in range(2):
                    for part, src in enumerate((part_hi[m], part_lo[m])):
                        row = (rep * 2 + part if which == "q" else part * 2 + rep) * DH0 + half * HALF0
                        sp.dma_start(rope_scratch[which][:, row:row + HALF0, :], src[:].bitcast(F32)).then_inc(stored, 16)
            sp.wait_ge(stored, 16 * 16)

        @block.scalar
        def _(act):
            act.wait_ge(w_in, 16)
            nc.scalar.copy(w_hi[:], w[:]).then_inc(w_hi_done, 1)
            norm.on_scalar(act)
            for c in range(KT):
                for n in range(NC):
                    act.wait_ge(transposed, c * NC + n + 1)
                    nc.scalar.copy(xT_hi[:, c, n * CH:(n + 1) * CH], bank[:, c * NC + n, :]).then_inc(xT_hi_done, 1)
            act.wait_ge(ffn_in, 80)
            nc.scalar.activation(up_sign[:], up[:], ACT.Sign).then_inc(signs_done, 1)
            nc.scalar.activation(down_sign[:], down[:], ACT.Sign).then_inc(signs_done, 1)
            for m in range(4):
                act.wait_ge(rope_step, STEPS * m + 3)
                nc.scalar.copy(part_hi[m][:], rot[0][:]).then_inc(rot_hi_done, 1)
            for n in range(NT // 2):
                act.wait_ge(v_projected, n + 1)
                nc.scalar.copy(v_sb[:, 2 * n:2 * n + 2, :],
                               bank[:, 4 + n, :].rearrange("p (j d) -> p j d", j=2)).then_inc(v_copied, 1)
            for n in range(NU):
                act.wait_ge(up_done, n + 1)
                if n >= 2:
                    act.wait_ge(hid_lo_done, n - 1)
                nc.scalar.activation(hid[n % 2][:], bank[:, n % 4, :], ACT.Relu,
                                     scale=up_scale[:, n % UT:n % UT + 1]).then_inc(relu_done, 1)

        @block.vector
        def _(dve):
            dve.wait_ge(x_in, 16)
            norm.on_vector(dve, x, xn)
            dve.wait_ge(const_in, 32)
            nc.vector.tensor_copy(ident_bf[:], ident[:]).then_inc(consts, 1)
            nc.vector.tensor_copy(mask_bf[:], mask[:]).then_inc(consts, 1)
            dve.wait_ge(w_hi_done, 1)
            nc.vector.tensor_tensor(w_lo[:], w[:], w_hi[:].bitcast(F32), ALU.subtract).then_inc(w_lo_done, 1)
            for c in range(KT):
                for n in range(NC):
                    dve.wait_ge(xT_hi_done, c * NC + n + 1)
                    cols = slice(n * CH, (n + 1) * CH)
                    nc.vector.tensor_tensor(xT_lo[:, c, cols], bank[:, c * NC + n, :],
                                            xT_hi[:, c, cols].bitcast(F32), ALU.subtract).then_inc(xT_lo_done, 1)
            dve.wait_ge(table_in, 64)
            done = 0
            for m in range(4):
                which, half = "qk"[m // 2], m % 2
                base = 4 if which == "q" else 0
                even = bank[:, base:base + 2, :].rearrange("p b t -> p (b t)")
                odd = bank[:, base + 2:base + 4, :].rearrange("p b t -> p (b t)")
                cos, sin = table["cos_" + which], table["sin_" + which]
                dve.wait_ge(projected, 4 * (m // 2) + 4)
                if m >= 1:
                    dve.wait_ge(rope_step, done)
                nc.vector.tensor_tensor(prod[0][:], even, (cos if half == 0 else sin)[:], ALU.mult).then_inc(rope_step, 1)
                nc.vector.tensor_tensor(prod[1][:], odd, (sin if half == 0 else cos)[:], ALU.mult).then_inc(rope_step, 1)
                dve.wait_ge(rope_step, done + 2)
                nc.vector.tensor_tensor(rot[0][:], prod[0][:], prod[1][:],
                                        ALU.subtract if half == 0 else ALU.add).then_inc(rope_step, 1)
                dve.wait_ge(rope_step, done + 3)
                dve.wait_ge(rot_hi_done, m + 1)
                nc.vector.tensor_tensor(part_lo[m][:], rot[0][:], part_hi[m][:].bitcast(F32),
                                        ALU.subtract).then_inc(rope_step, 1)
                done += STEPS

            def down_units(c):
                for n in range(c * TPC, (c + 1) * TPC):
                    dve.wait_ge(down_done, n + 1)
                    if n >= 2:
                        dve.wait_ge(x_added, n - 1)
                    nc.vector.tensor_tensor(scaled[n % 2][:], bank[:, 4 + n % 4, 0:D], down_scale[:],
                                            ALU.mult).then_inc(down_scaled, 1)
                    dve.wait_ge(down_scaled, n + 1)
                    nc.vector.scalar_tensor_tensor(x[:, n, :], scaled[n % 2][:], out_scale[:, 0:1], x[:, n, :],
                                                   ALU.mult, ALU.add).then_inc(x_added, 1)

            for c in range(NC):
                for u in range(UT):
                    n = c * UT + u
                    dve.wait_ge(relu_done, n + 1)
                    if c:
                        dve.wait_ge(down_done, c * TPC)
                    nc.vector.tensor_copy(hid_hi[:, u, :], hid[n % 2][:]).then_inc(hid_hi_done, 1)
                down_units(c)

        @block.gpsimd
        def _(pool):
            for n in range(NU):
                pool.wait_ge(hid_hi_done, n + 1)
                nc.gpsimd.tensor_tensor(hid_lo[:, n % UT, :], hid[n % 2][:],
                                        hid_hi[:, n % UT, :].bitcast(F32), ALU.subtract).then_inc(hid_lo_done, 1)

        @block.tensor
        def _(pe):
            pe.wait_ge(const_in, 32)
            for c in range(KT):
                for j in range(NT):
                    pe.wait_ge(norm.step, norm.DONE + (j + 1 if c == 0 else NT))
                    last = nc.tensor.transpose(bank[:, c * NC + j // TPC, (j % TPC) * P:(j % TPC + 1) * P],
                                               xn[:, j, c * P:(c + 1) * P], ident[:])
                    if j % TPC == TPC - 1:
                        last.then_inc(transposed, 1)
            pe.wait_ge(w_lo_done, 1)
            pe.wait_ge(xT_lo_done, KT * NC)
            for m in range(4):
                for c in range(NC):
                    out = bank[:, (4 + 2 * m + c) % 8, :]
                    cols = slice(c * CH, (c + 1) * CH)
                    for k in range(KT):
                        for n, (a, b) in enumerate(three((w_hi, xT_hi), (w_lo, xT_hi), (w_hi, xT_lo))):
                            last = nc.tensor.matmul(out, a[:, k, m * P:(m + 1) * P], b[:, k, cols],
                                                    start=(k == 0 and n == 0), stop=(k == KT - 1 and n == 2))
                    last.then_inc(projected, 1)
            for jj in range(NT // 2):
                pe.wait_ge(rope_step, 2 * STEPS)
                for j in (2 * jj, 2 * jj + 1):
                    out = bank[:, 4 + jj, (j % 2) * D:(j % 2 + 1) * D]
                    rows = slice(j * P, (j + 1) * P)
                    for k in range(KT):
                        for n, (a, b) in enumerate(three((xT_hi, w_hi), (xT_lo, w_hi), (xT_hi, w_lo))):
                            last = nc.tensor.matmul(out, a[:, k, rows], b[:, k, 2 * D:3 * D],
                                                    start=(k == 0 and n == 0), stop=(k == KT - 1 and n == 2))
                last.then_inc(v_projected, 1)
            pe.wait_ge(signs_done, 2)
            pe.wait_ge(rope_step, 4 * STEPS)
            pe.wait_ge(v_copied, NT // 2)
            for c in range(NC):
                for u in range(UT):
                    n = c * UT + u
                    if n >= 4:
                        pe.wait_ge(relu_done, n - 3)
                    for k in range(KT):
                        for q, b in enumerate((xT_hi, xT_lo)):
                            last = nc.tensor.matmul(bank[:, n % 4, :], up_sign[:, k, u * P:(u + 1) * P],
                                                    b[:, k, c * CH:(c + 1) * CH],
                                                    start=(k == 0 and q == 0), stop=(k == KT - 1 and q == 1))
                    last.then_inc(up_done, 1)
                for j in range(TPC):
                    n = c * TPC + j
                    pe.wait_ge(hid_lo_done, (c + 1) * UT)
                    if n >= 4:
                        pe.wait_ge(down_scaled, n - 3)
                    for u in range(UT):
                        for q, a in enumerate((hid_hi, hid_lo)):
                            last = nc.tensor.matmul(bank[:, 4 + n % 4, 0:D], a[:, u, j * P:(j + 1) * P],
                                                    down_sign[:, u, :], start=(u == 0 and q == 0),
                                                    stop=(u == UT - 1 and q == 1))
                    last.then_inc(down_done, 1)


def attend_layer0(nc, d, ctx, sb, bank, ident, ident_bf, mask_bf, v_sb, rope_scratch, heads_hi, heads_lo):
    sem = Semaphores(nc, ctx, "b_")

    def buf(name, shape, dt=F32):
        return sb("b_" + name, shape, dt, on=ctx)

    NP_ = 4
    LAG = 3
    SLOTS = GH * NT
    TUS = GH * NTU
    q_pair = [buf(f"q_pair{n}", [P, T], F32R) for n in range(2)]
    k_pair = [buf(f"k_pair{n}", [P, T], F32R) for n in range(2)]
    probs = [buf(f"probs{n}", [P, T]) for n in range(NP_)]
    neg_max, row_sum, row_inv = buf("neg_max", [P, SLOTS]), buf("row_sum", [P, SLOTS]), buf("row_inv", [P, SLOTS])
    probsT = [[buf(f"probsT{h}_{c}", [P, (c + 1) * TPC, CH]) for c in range(NC)] for h in range(GH)]
    v_group = buf("v_group", [P, NT, GH, 2 * DH0])

    pair_in = [sem(f"pair_in{n}") for n in range(2)]
    scored, maxed, exped, inverted, normed = sem("scored"), sem("maxed"), sem("exped"), sem("inverted"), sem("normed")
    transposed = sem("transposed")
    copied = [sem("copied_by_act"), sem("copied_by_dve")]
    v_cleared, v_ready, inverted_seen = sem("v_cleared"), sem("v_ready"), sem("inverted_seen")
    mixed, heads_hi_done, heads_lo_done = sem("mixed"), sem("heads_hi_done"), sem("heads_lo_done")

    stack = {n: rope_scratch[n].rearrange("(pair two) r t -> pair (two r) t", two=2) for n in "qk"}
    S_BANK, T_BANK, O_BANK = 0, 4, 6

    with nc.Block() as block:
        @block.sync
        def _(sp):
            def load(g, pr):
                src = {n: stack[n].rearrange("(g two) p t -> g two p t", two=2)[bass.ds(g, 1), pr, :, :]
                       .rearrange("g p t -> (g p) t") for n in "qk"}
                sp.dma_start(q_pair[pr][:].bitcast(F32), src["q"]).then_inc(pair_in[pr], 16)
                sp.dma_start(k_pair[pr][:].bitcast(F32), src["k"]).then_inc(pair_in[pr], 16)

            for pr in range(2):
                load(0, pr)
            with sp.Fori(0, NG - 1) as g:
                for pr in range(2):
                    sp.wait_ge(scored, g * SLOTS + (pr + 1) * (SLOTS // 2))
                    load(g + 1, pr)

        @block.gpsimd
        def _(pool):
            nc.gpsimd.memset(v_group[:], 0.0).then_inc(v_cleared, 1)
            with pool.Fori(0, NG) as g:
                pool.wait_ge(v_cleared, 1)
                pool.wait_ge(heads_lo_done, g * NC + 1)
                src = v_sb[:].rearrange("p j (g h e) -> p j g h e", g=NG, h=GH)[:, :, bass.ds(g, 1), :, :]
                nc.gpsimd.tensor_copy(v_group[:, :, :, 0:DH0], src.rearrange("p j g h e -> p j (g h) e")
                                      ).then_inc(v_ready, 1)
                for s in range(SLOTS):
                    i = s % NT
                    pool.wait_ge(inverted, g * SLOTS + s + 1)
                    pool.sem_inc(inverted_seen)
                    w = (i + 1) * P
                    nc.gpsimd.tensor_scalar(probs[s % NP_][:, 0:w], probs[s % NP_][:, 0:w], row_inv[:, s:s + 1], 1.0,
                                            ALU.mult, ALU.mult).then_inc(normed, 1)

        def evacuate(eng, copy, g, s, mine):
            h, i = s // NT, s % NT
            for tu in TU_OF[i]:
                n = h * NTU + tu
                if n % 2 != mine:
                    continue
                _, j, blocks = T_UNITS[tu]
                eng.wait_ge(transposed, g * TUS + n + 1)
                c, col = i // TPC, (i % TPC) * P
                copy(probsT[h][c][:, j:j + blocks, col:col + P],
                     bank[:, T_BANK + n % 2, 0:blocks * P].rearrange("p (b q) -> p b q", b=blocks)
                     ).then_inc(copied[mine], 1)

        @block.scalar
        def _(act):
            with act.Fori(0, NG) as g:
                for s in range(SLOTS):
                    i = s % NT
                    w = (i + 1) * P
                    act.wait_ge(maxed, g * SLOTS + s + 1)
                    if s >= NP_:
                        h4, i4 = (s - NP_) // NT, (s - NP_) % NT
                        act.wait_ge(transposed, g * TUS + h4 * NTU + TU_OF[i4][-1] + 1)
                    nc.scalar.activation(
                        probs[s % NP_][:, 0:w], bank[:, S_BANK + 2 * (s % 2):S_BANK + 2 * (s % 2) + 2, :]
                        .rearrange("p b t -> p (b t)")[:, 0:w], ACT.Exp, bias=neg_max[:, s:s + 1],
                        accum_out=row_sum[:, s:s + 1]).then_inc(exped, 1)
                    if s >= LAG:
                        evacuate(act, nc.scalar.copy, g, s - LAG, 0)
                for s in range(SLOTS - LAG, SLOTS):
                    evacuate(act, nc.scalar.copy, g, s, 0)
                for c in range(NC):
                    act.wait_ge(mixed, g * NC + c + 1)
                    out = heads_hi[:, bass.ds(g, 1), c * CH:(c + 1) * CH].rearrange("p g t -> p (g t)")
                    nc.scalar.copy(out, bank[:, O_BANK + c, :]).then_inc(heads_hi_done, 1)

        @block.vector
        def _(dve):
            dve.sem_inc(heads_lo_done)
            with dve.Fori(0, NG) as g:
                for s in range(SLOTS):
                    i = s % NT
                    w = (i + 1) * P
                    dve.wait_ge(scored, g * SLOTS + s + 1)
                    nc.vector.tensor_reduce(
                        neg_max[:, s:s + 1], bank[:, S_BANK + 2 * (s % 2):S_BANK + 2 * (s % 2) + 2, :]
                        .rearrange("p b t -> p (b t)")[:, 0:w], AX_X, ALU.max, negate=True).then_inc(maxed, 1)
                    if s >= LAG:
                        evacuate(dve, nc.vector.tensor_copy, g, s - LAG, 1)
                    dve.wait_ge(exped, g * SLOTS + s + 1)
                    nc.vector.reciprocal(row_inv[:, s:s + 1], row_sum[:, s:s + 1]).then_inc(inverted, 1)
                for s in range(SLOTS - LAG, SLOTS):
                    evacuate(dve, nc.vector.tensor_copy, g, s, 1)
                for c in range(NC):
                    dve.wait_ge(heads_hi_done, g * NC + c + 1)
                    cols = slice(c * CH, (c + 1) * CH)
                    nc.vector.tensor_tensor(heads_lo[:, bass.ds(g, 1), cols].rearrange("p g t -> p (g t)"),
                                            bank[:, O_BANK + c, :],
                                            heads_hi[:, bass.ds(g, 1), cols].rearrange("p g t -> p (g t)").bitcast(F32),
                                            ALU.subtract).then_inc(heads_lo_done, 1)

        @block.tensor
        def _(pe):
            def scores(g, s):
                h, i = s // NT, s % NT
                rows = slice((h % 2) * STACK, (h % 2 + 1) * STACK)
                if i == 0:
                    pe.wait_ge(pair_in[h // 2], g * 32 + 32)
                if s >= 2:
                    pe.wait_ge(exped, g * SLOTS + s - 1)
                for col, w in score_chunks(i):
                    out = bank[:, S_BANK + 2 * (s % 2) + col // CH, 0:w]
                    diagonal = col + w == (i + 1) * P
                    last = nc.tensor.matmul(out, q_pair[h // 2][rows, i * P:(i + 1) * P],
                                            k_pair[h // 2][rows, col:col + w], start=True, stop=not diagonal)
                    if diagonal:
                        last = nc.tensor.matmul(out[:, w - P:w], ident_bf[:], mask_bf[:], start=False, stop=True)
                last.then_inc(scored, 1)

            def transposes(g, s):
                h, i = s // NT, s % NT
                pe.wait_ge(normed, g * SLOTS + s + 1)
                for tu in TU_OF[i]:
                    n = h * NTU + tu
                    _, j, blocks = T_UNITS[tu]
                    if n >= 2:
                        pe.wait_ge(copied[n % 2], g * (TUS // 2) + n // 2)
                    for b in range(blocks):
                        last = nc.tensor.transpose(bank[:, T_BANK + n % 2, b * P:(b + 1) * P],
                                                   probs[s % NP_][:, (j + b) * P:(j + b + 1) * P], ident[:])
                    last.then_inc(transposed, 1)

            with pe.Fori(0, NG) as g:
                for s in range(SLOTS):
                    scores(g, s)
                    if s >= LAG:
                        transposes(g, s - LAG)
                for s in range(SLOTS - LAG, SLOTS):
                    transposes(g, s)
                pe.wait_ge(v_ready, g + 1)
                for n in range(2):
                    pe.wait_ge(copied[n], (g + 1) * (TUS // 2))
                for c in range(NC):
                    pieces = pv_pieces(c)
                    for j, q in pieces:
                        for h in range(GH):
                            last = nc.tensor.matmul(bank[32 * h:32 * h + 32, O_BANK + c, q:CH],
                                                    v_group[:, j, h, :], probsT[h][c][:, j, q:CH],
                                                    start=(j == 0), stop=(j == len(pieces) - 1))
                    last.then_inc(mixed, 1)


def join_layer0(nc, d, ctx, sb, bank, x, ident, heads_hi, heads_lo, xT_hi, xT_lo, acc, comb_scratch):
    sem = Semaphores(nc, ctx, "c_")

    def buf(name, shape, dt=F32):
        return sb("c_" + name, shape, dt, on=ctx)

    NR = NE + 2
    wo = buf("wo", [P, NG, D])
    wo_hi, wo_lo = buf("wo_hi", [P, NG, D], F32R), buf("wo_lo", [P, NG, D], F32R)
    wr = buf("wr", [P, KT, NR])
    wr_hi, wr_lo = buf("wr_hi", [P, KT, NR], F32R), buf("wr_lo", [P, KT, NR], F32R)
    iota = buf("iota", [P, NE])
    xn = buf("xn", [P, NT, D])
    norm = Norm(nc, sb, ctx, "c_")
    logits = buf("logits", [P, NT, NR])
    row = {n: buf(n, [P, NT, 1]) for n in ("mx", "sum", "inv", "sum4", "sum4e", "inv4", "ez", "ez1", "gate")}
    shifted, expd, soft, hit, hitw = (buf(n, [P, NT, NE]) for n in ("shifted", "expd", "soft", "hit", "hitw"))
    top, top_id = buf("top", [P, NT, 8]), buf("top_id", [P, NT, 8], U32)
    top_idf, top_w = buf("top_idf", [P, NT, 8]), buf("top_w", [P, NT, 8])
    comb = buf("comb", [P, NT, 64])
    combT = buf("combT", [64, T])

    w_in, w_hi_done, w_lo_done = sem("w_in"), sem("w_hi_done"), sem("w_lo_done")
    projected, joined = sem("projected"), sem("joined")
    x_transposed, acc_done, n_transposed, xT_hi_done, xT_lo_done = (
        sem("x_transposed"), sem("acc_done"), sem("n_transposed"), sem("xT_hi_done"), sem("xT_lo_done"))
    routed, logits_out, step, exps = sem("routed"), sem("logits_out"), sem("step"), sem("exps")
    comb_transposed, combT_done, stored = sem("comb_transposed"), sem("combT_done"), sem("stored")
    SHIFT_STEP = 2
    ROUTE_STEPS = SHIFT_STEP + 3 + 2 * NT + 6 + 3 * TOPK + 3

    with nc.Block() as block:
        @block.sync
        def _(sp):
            sp.dma_start(wo[:], d["wo0"]).then_inc(w_in, 16)
            sp.dma_start(wr[:], d["router"]).then_inc(w_in, 16)
            sp.dma_start(iota[:], d["iota"]).then_inc(w_in, 16)
            sp.wait_ge(combT_done, NC)
            sp.dma_start(comb_scratch, combT[0:NE + 1, :]).then_inc(stored, 16)
            sp.wait_ge(stored, 16)

        @block.scalar
        def _(act):
            act.wait_ge(w_in, 48)
            nc.scalar.copy(wo_hi[:], wo[:]).then_inc(w_hi_done, 1)
            nc.scalar.copy(wr_hi[:], wr[:]).then_inc(w_hi_done, 1)
            norm.on_scalar(act)
            for k in range(KT):
                for c in range(NC):
                    act.wait_ge(x_transposed, k * NC + c + 1)
                    nc.scalar.copy(acc[:, k, c * CH:(c + 1) * CH], bank[:, k * NC + c, :]).then_inc(acc_done, 1)
            for k in range(KT):
                for c in range(NC):
                    act.wait_ge(n_transposed, k * NC + c + 1)
                    nc.scalar.copy(xT_hi[:, k, c * CH:(c + 1) * CH], bank[:, 4 + k * NC + c, :]
                                   ).then_inc(xT_hi_done, 1)
            act.wait_ge(routed, 1)
            nc.scalar.copy(logits[:], bank[:, 0, 0:NT * NR].rearrange("p (j r) -> p j r", j=NT)
                           ).then_inc(logits_out, 1)
            act.wait_ge(step, SHIFT_STEP)
            nc.scalar.activation(expd[:], shifted[:], ACT.Exp).then_inc(exps, 1)
            act.wait_ge(logits_out, 1)
            nc.scalar.activation(row["ez"][:], logits[:, :, NE:NE + 1], ACT.Exp, scale=-1.0).then_inc(exps, 1)
            for c in range(NC):
                act.wait_ge(comb_transposed, c + 1)
                nc.scalar.copy(combT[:, c * CH:(c + 1) * CH], bank[0:64, 1 + c, :]).then_inc(combT_done, 1)

        @block.vector
        def _(dve):
            dve.wait_ge(w_hi_done, 1)
            nc.vector.tensor_tensor(wo_lo[:], wo[:], wo_hi[:].bitcast(F32), ALU.subtract).then_inc(w_lo_done, 1)
            dve.wait_ge(w_hi_done, 2)
            nc.vector.tensor_tensor(wr_lo[:], wr[:], wr_hi[:].bitcast(F32), ALU.subtract).then_inc(w_lo_done, 1)
            for j in range(NT):
                dve.wait_ge(projected, j + 1)
                nc.vector.tensor_tensor(x[:, j, :], bank[:, j, 0:D], x[:, j, :], ALU.add).then_inc(joined, 1)
            dve.wait_ge(joined, NT)
            norm.on_vector(dve, x, xn)
            for k in range(KT):
                for c in range(NC):
                    dve.wait_ge(xT_hi_done, k * NC + c + 1)
                    cols = slice(c * CH, (c + 1) * CH)
                    nc.vector.tensor_tensor(xT_lo[:, k, cols], bank[:, 4 + k * NC + c, :],
                                            xT_hi[:, k, cols].bitcast(F32), ALU.subtract).then_inc(xT_lo_done, 1)

            count = [0]

            def chained(ins):
                ins.then_inc(step, 1)
                count[0] += 1
                dve.wait_ge(step, count[0])

            dve.wait_ge(logits_out, 1)
            experts = logits[:, :, 0:NE]
            chained(nc.vector.tensor_reduce(row["mx"][:], experts, AX_X, ALU.max))
            chained(nc.vector.tensor_tensor(shifted[:], experts, row["mx"][:].to_broadcast([P, NT, NE]), ALU.subtract))
            assert count[0] == SHIFT_STEP
            dve.wait_ge(exps, 1)
            chained(nc.vector.tensor_reduce(row["sum"][:], expd[:], AX_X, ALU.add))
            chained(nc.vector.reciprocal(row["inv"][:], row["sum"][:]))
            chained(nc.vector.tensor_tensor(soft[:], expd[:], row["inv"][:].to_broadcast([P, NT, NE]), ALU.mult))
            for j in range(NT):
                chained(nc.vector.max(top[:, j, :], soft[:, j, :]))
            for j in range(NT):
                chained(nc.vector.max_index(top_id[:, j, :], top[:, j, :], soft[:, j, :]))
            chained(nc.vector.tensor_copy(top_idf[:], top_id[:]))
            chained(nc.vector.tensor_reduce(row["sum4"][:], top[:, :, 0:TOPK], AX_X, ALU.add))
            chained(nc.vector.tensor_scalar(row["sum4e"][:], row["sum4"][:], 1e-20, None, ALU.add))
            chained(nc.vector.reciprocal(row["inv4"][:], row["sum4e"][:]))
            chained(nc.vector.scalar_tensor_tensor(top_w[:, :, 0:TOPK], top[:, :, 0:TOPK], 0.5,
                                                   row["inv4"][:].to_broadcast([P, NT, TOPK]), ALU.mult, ALU.mult))
            chained(nc.vector.memset(comb[:], 0.0))
            for k in range(TOPK):
                chained(nc.vector.tensor_tensor(
                    hit[:], iota[:].rearrange("p (o e) -> p o e", o=1).to_broadcast([P, NT, NE]),
                    top_idf[:, :, k:k + 1].to_broadcast([P, NT, NE]), ALU.is_equal))
                chained(nc.vector.tensor_tensor(hitw[:], hit[:], top_w[:, :, k:k + 1].to_broadcast([P, NT, NE]), ALU.mult))
                chained(nc.vector.tensor_tensor(comb[:, :, 0:NE], comb[:, :, 0:NE], hitw[:], ALU.add))
            dve.wait_ge(exps, 2)
            chained(nc.vector.tensor_scalar(row["ez1"][:], row["ez"][:], 1.0, None, ALU.add))
            chained(nc.vector.reciprocal(row["gate"][:], row["ez1"][:]))
            chained(nc.vector.tensor_scalar(comb[:, :, NE:NE + 1], row["gate"][:], 0.5, None, ALU.mult))
            assert count[0] == ROUTE_STEPS

        @block.tensor
        def _(pe):
            pe.wait_ge(w_lo_done, 1)
            for j in range(NT):
                rows = slice(j * P, (j + 1) * P)
                for g in range(NG):
                    for n, (a, b) in enumerate(three((heads_hi, wo_hi), (heads_lo, wo_hi), (heads_hi, wo_lo))):
                        last = nc.tensor.matmul(bank[:, j, 0:D], a[:, g, rows], b[:, g, :],
                                                start=(g == 0 and n == 0), stop=(g == NG - 1 and n == 2))
                last.then_inc(projected, 1)

            def transpose_all(src, first, done, ready):
                for k in range(KT):
                    for j in range(NT):
                        ready(k, j)
                        last = nc.tensor.transpose(bank[:, first + k * NC + j // TPC, (j % TPC) * P:(j % TPC + 1) * P],
                                                   src[:, j, k * P:(k + 1) * P], ident[:])
                        if j % TPC == TPC - 1:
                            last.then_inc(done, 1)

            transpose_all(x, 0, x_transposed, lambda k, j: pe.wait_ge(joined, NT))
            transpose_all(xn, 4, n_transposed,
                          lambda k, j: pe.wait_ge(norm.step, norm.DONE + (j + 1 if k == 0 else NT)))
            pe.wait_ge(xT_lo_done, KT * NC)
            pe.wait_ge(w_lo_done, 2)
            pe.wait_ge(acc_done, 1)
            for j in range(NT):
                rows = slice(j * P, (j + 1) * P)
                for k in range(KT):
                    for n, (a, b) in enumerate(three((xT_hi, wr_hi), (xT_lo, wr_hi), (xT_hi, wr_lo))):
                        last = nc.tensor.matmul(bank[:, 0, j * NR:(j + 1) * NR], a[:, k, rows], b[:, k, :],
                                                start=(k == 0 and n == 0), stop=(k == KT - 1 and n == 2))
            last.then_inc(routed, 1)
            pe.wait_ge(step, ROUTE_STEPS)
            pe.wait_ge(acc_done, 3)
            for j in range(NT):
                last = nc.tensor.transpose(bank[0:64, 1 + j // TPC, (j % TPC) * P:(j % TPC + 1) * P],
                                           comb[:, j, :], ident[:])
                if j % TPC == TPC - 1:
                    last.then_inc(comb_transposed, 1)


def layer1(nc, d, ctx, sb, bank, ident, ident_bf, mask_bf, xT_hi, xT_lo, acc, comb_scratch):
    sem = Semaphores(nc, ctx, "d_")

    def buf(name, shape, dt=F32):
        return sb("d_" + name, shape, dt, on=ctx)

    QKV, GU = KT * 3 * P, KT * 2 * P
    cos, sin = buf("cos", [P, T]), buf("sin", [P, T])
    gl, ge, g1, gs = buf("gl", [P, H1]), buf("ge", [P, H1]), buf("g1", [P, H1]), buf("gs", [P, H1])
    gs_now = buf("gs_now", [P, 1])
    qkv_raw, qkv_hi, qkv_lo = buf("qkv_raw", [P, QKV]), buf("qkv_hi", [P, QKV], F32R), buf("qkv_lo", [P, QKV], F32R)
    gu_raw, gu_hi, gu_lo = buf("gu_raw", [P, GU]), buf("gu_hi", [P, GU], F32R), buf("gu_lo", [P, GU], F32R)
    ow_raw = buf("ow_raw", [P, 3, D])
    ow_hi, ow_lo = buf("ow_hi", [P, 3, D], F32R), buf("ow_lo", [P, 3, D], F32R)
    cb = buf("cb", [P, T])
    qk_hi = {w: buf(f"{w}_hi", [P, T], F32R) for w in "qk"}
    qk_lo = {w: buf(f"{w}_lo", [P, T], F32R) for w in "qk"}
    swap = [buf(f"swap{n}", [P, CH]) for n in range(2)]
    rot = [buf(f"rot{n}", [P, CH]) for n in range(2)]
    v_hi, v_lo = buf("v_hi", [P, NT, DV], F32R), buf("v_lo", [P, NT, DV], F32R)
    NP_ = 4
    probs = [buf(f"probs{n}", [P, T]) for n in range(NP_)]
    neg_max, row_sum, row_inv = (buf(n, [P, HPI * NT]) for n in ("neg_max", "row_sum", "row_inv"))
    pT_hi = [buf(f"pT_hi{c}", [P, (c + 1) * TPC, CH], F32R) for c in range(NC)]
    pT_lo = [buf(f"pT_lo{c}", [P, (c + 1) * TPC, CH], F32R) for c in range(NC)]
    head_hi, head_lo = buf("head_hi", [P, T], F32R), buf("head_lo", [P, T], F32R)
    tanh = [buf(f"tanh{n}", [P, CH]) for n in range(2)]
    g_act, gu_act = buf("g_act", [P, CH]), buf("gu_act", [P, CH])
    hid = [buf(f"hid{n}", [P, CH]) for n in range(2)]
    hid_hi, hid_lo = buf("hid_hi", [P, 2, T], F32R), buf("hid_lo", [P, 2, T], F32R)

    const_in, gate_step = sem("const_in"), sem("gate_step")
    qkv_in, gu_in, ow_in, cb_in = sem("qkv_in"), sem("gu_in"), sem("ow_in"), sem("cb_in")
    qkv_hi_done, qkv_lo_done, gu_hi_done, gu_lo_done, ow_hi_done, ow_lo_done = (
        sem(n) for n in ("qkv_hi_done", "qkv_lo_done", "gu_hi_done", "gu_lo_done", "ow_hi_done", "ow_lo_done"))
    unit_done = sem("unit_done")
    unit_free = sem("unit_free")
    swapped, sin_done, rotated, qk_hi_done, qk_lo_done = (
        sem(n) for n in ("swapped", "sin_done", "rotated", "qk_hi_done", "qk_lo_done"))
    swap_cleared = sem("swap_cleared")
    v_hi_done, inverted_seen = sem("v_hi_done"), sem("inverted_seen")
    scored, maxed, exped, inverted, normed = (sem(n) for n in ("scored", "maxed", "exped", "inverted", "normed"))
    transposed, pT_hi_done, pT_lo_done = sem("transposed"), sem("pT_hi_done"), sem("pT_lo_done")
    head_hi_done = sem("head_hi_done")
    tanh_done, hid_done, hid_hi_done, hid_lo_done = (
        sem(n) for n in ("tanh_done", "hid_done", "hid_hi_done", "hid_lo_done"))
    out_done = sem("out_done")

    S_BANK, T_BANK, U_BANK = 0, 4, 6

    SHARED_UNITS = 2 * (2 * 2 * NC + KT * NC)
    SHARED_PAIRS = ST * NC
    QK_UNITS, V_UNITS, PV_UNITS, OUT_UNITS = 2 * NC, NT // TPC, NC, KT * NC
    LOOP0 = SHARED_UNITS + QK_UNITS
    PAIRS = [[(0, 0), (0, 1), (1, 0)], [(1, 1), (2, 0), (2, 1)]]
    PAIR_SLOTS = [1, 3, 5]
    NPAIR = len(PAIR_SLOTS)
    HEAD_UNITS = V_UNITS + 2 * NPAIR + QK_UNITS + PV_UNITS + OUT_UNITS
    ROUND_UNITS = HPI * HEAD_UNITS
    HID_BUF = [0, 1, 0]
    OUT_TILES = [[0], [1, 2]]
    OW = [1 + len(t) for t in OUT_TILES]
    LAG = 2

    class Head:

        def __init__(self, it, hh, last):
            self.hh, self.last_head = hh, last and hh == HPI - 1
            self.h = it * HPI + hh
            self.unit = it * ROUND_UNITS + (LOOP0 + hh * HEAD_UNITS)
            self.slot = it * (HPI * NT) + hh * NT
            self.tu = it * (HPI * NTU) + hh * NTU
            self.pair = it * (HPI * NPAIR) + (SHARED_PAIRS + hh * NPAIR)
            self.v0 = self.unit
            self.pairs0 = self.unit + V_UNITS
            self.next_qk0 = self.pairs0 + 2 * NPAIR
            self.pv0 = self.next_qk0 + (0 if self.last_head else QK_UNITS)
            self.out0 = self.pv0 + PV_UNITS
            self.next_qk = it * (HPI * QK_UNITS) + (hh + 1) * QK_UNITS
            self.tile = it * ET

    def unit_bank(n):
        return bank[:, U_BANK + n % 2, :]

    assert SHARED_UNITS % 2 == 0 and HEAD_UNITS % 2 == 0 and QK_UNITS % 2 == 0

    def rounds(engine, body):
        with engine.Fori(0, NEG - 1) as it:
            for hh in range(HPI):
                body(Head(it, hh, False), it)
        for hh in range(HPI):
            body(Head(NEG - 1, hh, True), NEG - 1)

    GU_SPLIT = {(0, 4): 1, (1, 2): 2, (1, 6): ET}
    QKV_SLOT, OW_SLOT = 3, 2

    with nc.Block() as block:
        @block.sync
        def _(sp):
            sp.dma_start(cos[:], d["cos1"]).then_inc(const_in, 16)
            sp.dma_start(sin[:], d["sin1"]).then_inc(const_in, 16)
            sp.dma_start(gl[:], d["gate_logit"]).then_inc(const_in, 16)
            sp.dma_start(cb[:], comb_scratch[NE:NE + 1, :].to_broadcast([P, T])).then_inc(cb_in, 16)
            for t in range(ST):
                if t:
                    sp.wait_ge(gu_hi_done, t)
                    sp.wait_ge(gu_lo_done, t)
                sp.dma_start(gu_raw[:], d["gu_shared"][t]).then_inc(gu_in, 16)
                if t % 2 == 0:
                    if t:
                        sp.wait_ge(ow_hi_done, t // 2)
                        sp.wait_ge(ow_lo_done, t // 2)
                    sp.dma_start(ow_raw[:, 0:2, :], d["down_shared"][t // 2]).then_inc(ow_in, 16)
            sp.dma_start(qkv_raw[:], d["w_qkv1"][0]).then_inc(qkv_in, 16)
            sp.wait_ge(gu_hi_done, ST)
            sp.wait_ge(gu_lo_done, ST)
            sp.dma_start(gu_raw[:], d["gu1"][0]).then_inc(gu_in, 16)

            def body(h, it):
                if h.hh == 0:
                    sp.wait_ge(hid_done, h.pair)
                    src = d_comb[bass.ds(it, 1)].rearrange("o e r t -> (o e) r t")
                    sp.dma_start(cb[:], src).then_inc(cb_in, 16)
                sp.wait_ge(ow_hi_done, h.h + ST // 2)
                sp.wait_ge(ow_lo_done, h.h + ST // 2)
                src = (d["ow_a"] if h.hh == 0 else d["ow_b"])[bass.ds(it, 1)].rearrange("o p t n -> (o p) t n")
                sp.dma_start(ow_raw[:, 0:OW[h.hh], :], src).then_inc(ow_in, 16)
                if not h.last_head:
                    sp.wait_ge(qkv_hi_done, h.h + 1)
                    sp.wait_ge(qkv_lo_done, h.h + 1)
                    sp.dma_start(qkv_raw[:], d["w_qkv1"][bass.ds(h.h + 1, 1)].rearrange("o p n -> (o p) n")
                                 ).then_inc(qkv_in, 16)
                for s in range(NT):
                    t = GU_SPLIT.get((h.hh, s))
                    if t is None or (t == ET and h.last_head):
                        continue
                    sp.wait_ge(gu_hi_done, h.tile + ST + t)
                    sp.wait_ge(gu_lo_done, h.tile + ST + t)
                    sp.dma_start(gu_raw[:], d["gu1"][bass.ds(h.tile + t, 1)].rearrange("o p n -> (o p) n")
                                 ).then_inc(gu_in, 16)

            d_comb = comb_scratch[0:NE, :].rearrange("(g e o) t -> g e o t", e=EG, o=1).to_broadcast(
                [NEG, EG, P // EG, T])
            rounds(sp, body)
            sp.wait_ge(unit_free, Head(NEG - 1, HPI - 1, True).out0 + OUT_UNITS)
            for k in range(KT):
                sp.dma_start(d["out"][k], acc[:, k, :]).then_inc(out_done, 16)
            sp.wait_ge(out_done, 16 * KT)

        @block.scalar
        def _(act):
            def part_hi(dst, src, raw_in, raw_n, used_units, done):
                act.wait_ge(raw_in, raw_n)
                act.wait_ge(unit_done, used_units)
                nc.scalar.copy(dst, src).then_inc(done, 1)

            act.wait_ge(const_in, 48)
            nc.scalar.activation(ge[:], gl[:], ACT.Exp, scale=-1.0).then_inc(gate_step, 1)

            def hidden_hi(pair, par, buf_n, c, out_free):
                act.wait_ge(hid_done, pair + 1)
                act.wait_ge(unit_done, out_free)
                nc.scalar.copy(hid_hi[:, buf_n, c * CH:(c + 1) * CH], hid[par][:]).then_inc(hid_hi_done, 1)

            def qk_units(first_unit, first, gate):
                def hi(n):
                    w, c = "qk"[n // NC], n % NC
                    act.wait_ge(rotated, first + n + 1)
                    nc.scalar.copy(qk_hi[w][:, c * CH:(c + 1) * CH], rot[n % 2][:]).then_inc(qk_hi_done, 1)

                for n in range(QK_UNITS):
                    act.wait_ge(unit_done, first_unit + n + 1)
                    if n >= 2:
                        act.wait_ge(rotated, first + n - 1)
                    for dst, src in ((DS, DS + 32), (DS + 32, DS)):
                        last = nc.scalar.activation(
                            swap[n % 2][dst:dst + 32, :], unit_bank(n)[src:src + 32, :], ACT.Copy,
                            scale=gs_now[src:src + 32, :] if n < NC else 1.0)
                    last.then_inc(swapped, 1)
                    if n >= 1:
                        hi(n - 1)
                hi(QK_UNITS - 1)

            def shared_half(a):
                for t in (2 * a, 2 * a + 1):
                    u0 = a * (SHARED_UNITS // 2) + (t % 2) * 2 * NC
                    part_hi(gu_hi[:], gu_raw[:], gu_in, 16 * (t + 1), u0 - (OUT_UNITS if t % 2 == 0 and a else 0), gu_hi_done)
                    for c in range(NC):
                        p = t * NC + c
                        act.wait_ge(unit_done, u0 + 2 * c + 1)
                        if p >= 2:
                            act.wait_ge(hid_done, p - 1)
                        nc.scalar.activation(tanh[p % 2][:], unit_bank(0), ACT.Tanh, scale=0.5).then_inc(tanh_done, 1)
                        hidden_hi(p, p % 2, t % 2, c, a * (SHARED_UNITS // 2))
                part_hi(ow_hi[:, 0:2, :], ow_raw[:, 0:2, :], ow_in, 16 * (a + 1), a * (SHARED_UNITS // 2), ow_hi_done)

            for a in range(2):
                shared_half(a)
            part_hi(qkv_hi[:], qkv_raw[:], qkv_in, 16, 0, qkv_hi_done)
            part_hi(gu_hi[:], gu_raw[:], gu_in, 16 * (ST + 1), SHARED_UNITS - OUT_UNITS, gu_hi_done)
            act.wait_ge(gate_step, 5)
            qk_units(SHARED_UNITS, 0, None)

            def pT_parts(h, i):
                for tu in TU_OF[i]:
                    _, j, blocks = T_UNITS[tu]
                    c, col = i // TPC, (i % TPC) * P
                    act.wait_ge(transposed, h.tu + tu + 1)
                    nc.scalar.copy(pT_hi[c][:, j:j + blocks, col:col + P],
                                   bank[:, T_BANK + tu % 2, 0:blocks * P].rearrange("p (b q) -> p b q", b=blocks)
                                   ).then_inc(pT_hi_done, 1)

            def body(h, it):
                for n in range(V_UNITS):
                    act.wait_ge(unit_done, h.v0 + n + 1)
                    nc.scalar.copy(v_hi[:, n * TPC:(n + 1) * TPC, :],
                                   unit_bank(n).rearrange("p (j e) -> p j e", j=TPC)).then_inc(v_hi_done, 1)

                def hidden(n):
                    tile, c = PAIRS[h.hh][n]
                    free = {0: h.unit, 1: h.unit - (HEAD_UNITS if h.hh else 0), 2: h.unit}[tile]
                    hidden_hi(h.pair + n, (h.hh + n) % 2, HID_BUF[tile], c, free)

                for s in range(NT):
                    w = (s + 1) * P
                    act.wait_ge(maxed, h.slot + s + 1)
                    if s >= NP_:
                        act.wait_ge(transposed, h.tu + TU_OF[s - NP_][-1] + 1)
                    nc.scalar.activation(
                        probs[s % NP_][:, 0:w],
                        bank[:, S_BANK + 2 * (s % 2):S_BANK + 2 * (s % 2) + 2, :].rearrange("p b t -> p (b t)")[:, 0:w],
                        ACT.Exp, bias=neg_max[:, h.hh * NT + s:h.hh * NT + s + 1],
                        accum_out=row_sum[:, h.hh * NT + s:h.hh * NT + s + 1]).then_inc(exped, 1)
                    if s >= LAG:
                        pT_parts(h, s - LAG)
                    if s - 1 in PAIR_SLOTS:
                        hidden(PAIR_SLOTS.index(s - 1))
                    if s in PAIR_SLOTS:
                        n = PAIR_SLOTS.index(s)
                        act.wait_ge(unit_done, h.pairs0 + 2 * n + 1)
                        act.wait_ge(hid_done, h.pair + n - 1)
                        nc.scalar.activation(tanh[(h.hh + n) % 2][:], unit_bank(0), ACT.Tanh, scale=0.5
                                             ).then_inc(tanh_done, 1)
                    if s == OW_SLOT:
                        part_hi(ow_hi[:, 0:OW[h.hh], :], ow_raw[:, 0:OW[h.hh], :], ow_in,
                                (h.h + ST // 2) * 16 + 16, h.unit, ow_hi_done)
                    if s == QKV_SLOT and not h.last_head:
                        part_hi(qkv_hi[:], qkv_raw[:], qkv_in, h.h * 16 + 32, h.v0 + V_UNITS, qkv_hi_done)
                    t = GU_SPLIT.get((h.hh, s))
                    if t is not None and not (t == ET and h.last_head):
                        used = h.pairs0 + 2 * sum(1 for q in PAIR_SLOTS if q < s)
                        part_hi(gu_hi[:], gu_raw[:], gu_in, (h.tile + ST + t) * 16 + 16, used, gu_hi_done)
                if not h.last_head:
                    act.wait_ge(gate_step, h.h + 6)
                    qk_units(h.next_qk0, h.next_qk, True)
                for i in range(NT - LAG, NT):
                    pT_parts(h, i)
                for c in range(PV_UNITS):
                    act.wait_ge(unit_done, h.pv0 + c + 1)
                    nc.scalar.copy(head_hi[:, c * CH:(c + 1) * CH], unit_bank(c)).then_inc(head_hi_done, 1)

            rounds(act, body)

        @block.vector
        def _(dve):
            def pair_steps(pair, tanh_par, first_unit):
                c = pair[1]
                dve.wait_ge(tanh_done, pair[0] + 1)
                dve.wait_ge(hid_done, pair[0])
                nc.vector.scalar_tensor_tensor(g_act[:], tanh[tanh_par][:], 1.0, unit_bank(0), ALU.add, ALU.mult
                                               ).then_inc(unit_free, 1)
                dve.wait_ge(unit_done, first_unit + 2)
                dve.wait_ge(unit_free, first_unit + 1)
                nc.vector.tensor_tensor(gu_act[:], g_act[:], unit_bank(1), ALU.mult).then_inc(unit_free, 1)
                dve.wait_ge(unit_free, first_unit + 2)
                dve.wait_ge(hid_lo_done, pair[2])
                nc.vector.tensor_tensor(hid[tanh_par][:], gu_act[:], cb[:, c * CH:(c + 1) * CH], ALU.mult
                                        ).then_inc(hid_done, 1)

            def out_units(first):
                for n in range(OUT_UNITS):
                    k, c = n // NC, n % NC
                    dve.wait_ge(unit_done, first + n + 1)
                    dve.wait_ge(unit_free, first + n)
                    nc.vector.tensor_tensor(acc[:, k, c * CH:(c + 1) * CH], acc[:, k, c * CH:(c + 1) * CH],
                                            unit_bank(n), ALU.add).then_inc(unit_free, 1)

            def qk_units(first_unit, first, gate_n):
                def add(n):
                    dve.wait_ge(sin_done, first + n + 1)
                    dve.wait_ge(unit_free, first_unit + n + 1)
                    nc.vector.tensor_tensor(rot[n % 2][DS:P, :], rot[n % 2][DS:P, :], swap[n % 2][DS:P, :], ALU.add
                                            ).then_inc(rotated, 1)

                for n in range(QK_UNITS):
                    c = n % NC
                    dve.wait_ge(swapped, first + n + 1)
                    if n >= 2:
                        dve.wait_ge(qk_lo_done, first + n - 1)
                    if n < NC:
                        nc.vector.scalar_tensor_tensor(rot[n % 2][:], unit_bank(n), gs_now[:, 0:1],
                                                       cos[:, c * CH:(c + 1) * CH], ALU.mult, ALU.mult
                                                       ).then_inc(unit_free, 1)
                    else:
                        nc.vector.tensor_tensor(rot[n % 2][:], unit_bank(n), cos[:, c * CH:(c + 1) * CH], ALU.mult
                                                ).then_inc(unit_free, 1)
                    if n >= 1:
                        add(n - 1)
                add(QK_UNITS - 1)

            for n in range(2):
                nc.vector.memset(swap[n][0:DS, :], 0.0).then_inc(swap_cleared, 1)
            scale = float(DS) ** -0.5
            dve.wait_ge(gate_step, 1)
            nc.vector.tensor_scalar(g1[:], ge[:], 1.0, None, ALU.add).then_inc(gate_step, 1)
            dve.wait_ge(gate_step, 2)
            nc.vector.reciprocal(ge[:], g1[:]).then_inc(gate_step, 1)
            dve.wait_ge(gate_step, 3)
            nc.vector.tensor_scalar(gs[0:DS, :], ge[0:DS, :], scale, None, ALU.mult)
            nc.vector.tensor_scalar(gs[DS:P, :], ge[DS:P, :], -scale, scale, ALU.mult, ALU.add).then_inc(gate_step, 1)
            dve.wait_ge(gate_step, 4)
            nc.vector.tensor_copy(gs_now[:], gs[:, 0:1]).then_inc(gate_step, 1)

            for a in range(2):
                half = a * (SHARED_UNITS // 2)
                dve.wait_ge(cb_in, 16)
                for q in range(2 * NC):
                    p = a * 2 * NC + q
                    pair_steps((p, q % NC, max(0, p - 1)), p % 2, half + 2 * q)
                out_units(half + 4 * NC)
            dve.wait_ge(gate_step, 5)
            qk_units(SHARED_UNITS, 0, 0)

            def pT_parts(h, i):
                for tu in TU_OF[i]:
                    _, j, blocks = T_UNITS[tu]
                    c, col = i // TPC, (i % TPC) * P
                    dve.wait_ge(pT_hi_done, h.tu + tu + 1)
                    nc.vector.tensor_tensor(pT_lo[c][:, j:j + blocks, col:col + P],
                                            bank[:, T_BANK + tu % 2, 0:blocks * P].rearrange("p (b q) -> p b q", b=blocks),
                                            pT_hi[c][:, j:j + blocks, col:col + P].bitcast(F32), ALU.subtract
                                            ).then_inc(pT_lo_done, 1)

            def body(h, it):
                for n in range(V_UNITS):
                    dve.wait_ge(v_hi_done, h.h * V_UNITS + n + 1)
                    nc.vector.tensor_tensor(v_lo[:, n * TPC:(n + 1) * TPC, :],
                                            unit_bank(n).rearrange("p (j e) -> p j e", j=TPC),
                                            v_hi[:, n * TPC:(n + 1) * TPC, :].bitcast(F32), ALU.subtract
                                            ).then_inc(unit_free, 1)
                if h.hh == 0:
                    dve.wait_ge(cb_in, it * 16 + 32)
                for s in range(NT):
                    w = (s + 1) * P
                    col = slice(h.hh * NT + s, h.hh * NT + s + 1)
                    dve.wait_ge(scored, h.slot + s + 1)
                    nc.vector.tensor_reduce(
                        neg_max[:, col],
                        bank[:, S_BANK + 2 * (s % 2):S_BANK + 2 * (s % 2) + 2, :].rearrange("p b t -> p (b t)")[:, 0:w],
                        AX_X, ALU.max, negate=True).then_inc(maxed, 1)
                    if s >= LAG:
                        pT_parts(h, s - LAG)
                    dve.wait_ge(exped, h.slot + s + 1)
                    nc.vector.reciprocal(row_inv[:, col], row_sum[:, col]).then_inc(inverted, 1)
                    if s in PAIR_SLOTS:
                        n = PAIR_SLOTS.index(s)
                        pair_steps((h.pair + n, PAIRS[h.hh][n][1], h.pair + n - 1), (h.hh + n) % 2,
                                   h.pairs0 + 2 * n)
                if not h.last_head:
                    dve.wait_ge(qk_hi_done, h.next_qk)
                    dve.wait_ge(gate_step, h.h + 5)
                    nc.vector.tensor_copy(gs_now[:], gs[:, bass.ds(h.h + 1, 1)]).then_inc(gate_step, 1)
                    dve.wait_ge(gate_step, h.h + 6)
                    qk_units(h.next_qk0, h.next_qk, None)
                for i in range(NT - LAG, NT):
                    pT_parts(h, i)
                for c in range(PV_UNITS):
                    dve.wait_ge(head_hi_done, h.h * PV_UNITS + c + 1)
                    cols = slice(c * CH, (c + 1) * CH)
                    nc.vector.tensor_tensor(head_lo[:, cols], unit_bank(c), head_hi[:, cols].bitcast(F32), ALU.subtract
                                            ).then_inc(unit_free, 1)
                out_units(h.out0)

            rounds(dve, body)

        @block.gpsimd
        def _(pool):
            def part_lo(dst, src, hi, hi_done, n, done):
                pool.wait_ge(hi_done, n)
                nc.gpsimd.tensor_tensor(dst, src, hi.bitcast(F32), ALU.subtract).then_inc(done, 1)

            def hidden_lo(pair, par, buf_n, c):
                pool.wait_ge(hid_hi_done, pair + 1)
                cols = slice(c * CH, (c + 1) * CH)
                nc.gpsimd.tensor_tensor(hid_lo[:, buf_n, cols], hid[par][:], hid_hi[:, buf_n, cols].bitcast(F32),
                                        ALU.subtract).then_inc(hid_lo_done, 1)

            def qk_units(first):
                def lo(n):
                    w, c = "qk"[n // NC], n % NC
                    cols = slice(c * CH, (c + 1) * CH)
                    pool.wait_ge(qk_hi_done, first + n + 1)
                    nc.gpsimd.tensor_tensor(qk_lo[w][:, cols], rot[n % 2][:], qk_hi[w][:, cols].bitcast(F32),
                                            ALU.subtract).then_inc(qk_lo_done, 1)

                for n in range(QK_UNITS):
                    c = n % NC
                    pool.wait_ge(swapped, first + n + 1)
                    nc.gpsimd.tensor_tensor(swap[n % 2][:], swap[n % 2][:], sin[:, c * CH:(c + 1) * CH],
                                            ALU.mult).then_inc(sin_done, 1)
                    if n >= 1:
                        lo(n - 1)
                lo(QK_UNITS - 1)

            for a in range(2):
                for t in (2 * a, 2 * a + 1):
                    part_lo(gu_lo[:], gu_raw[:], gu_hi[:], gu_hi_done, t + 1, gu_lo_done)
                    for c in range(NC):
                        hidden_lo(t * NC + c, (t * NC + c) % 2, t % 2, c)
                part_lo(ow_lo[:, 0:2, :], ow_raw[:, 0:2, :], ow_hi[:, 0:2, :], ow_hi_done, a + 1, ow_lo_done)
            part_lo(qkv_lo[:], qkv_raw[:], qkv_hi[:], qkv_hi_done, 1, qkv_lo_done)
            part_lo(gu_lo[:], gu_raw[:], gu_hi[:], gu_hi_done, ST + 1, gu_lo_done)
            pool.wait_ge(swap_cleared, 2)
            qk_units(0)

            def body(h, it):
                for s in range(NT):
                    w = (s + 1) * P
                    pool.wait_ge(inverted, h.slot + s + 1)
                    pool.sem_inc(inverted_seen)
                    nc.gpsimd.tensor_scalar(probs[s % NP_][:, 0:w], probs[s % NP_][:, 0:w],
                                            row_inv[:, h.hh * NT + s:h.hh * NT + s + 1], 1.0, ALU.mult, ALU.mult
                                            ).then_inc(normed, 1)
                    if s - 1 in PAIR_SLOTS:
                        n = PAIR_SLOTS.index(s - 1)
                        tile, c = PAIRS[h.hh][n]
                        hidden_lo(h.pair + n, (h.hh + n) % 2, HID_BUF[tile], c)
                    if s == OW_SLOT:
                        blocks = slice(0, OW[h.hh])
                        part_lo(ow_lo[:, blocks, :], ow_raw[:, blocks, :], ow_hi[:, blocks, :], ow_hi_done,
                                h.h + ST // 2 + 1, ow_lo_done)
                    if s == QKV_SLOT and not h.last_head:
                        part_lo(qkv_lo[:], qkv_raw[:], qkv_hi[:], qkv_hi_done, h.h + 2, qkv_lo_done)
                    t = GU_SPLIT.get((h.hh, s))
                    if t is not None and not (t == ET and h.last_head):
                        part_lo(gu_lo[:], gu_raw[:], gu_hi[:], gu_hi_done, h.tile + ST + t + 1, gu_lo_done)
                if not h.last_head:
                    qk_units(h.next_qk)

            rounds(pool, body)

        @block.tensor
        def _(pe):
            def w_slice(w, k, part):
                return w[:, (k * 3 + part) * P:(k * 3 + part + 1) * P]

            def gu_slice(w, k, part):
                return w[:, (k * 2 + part) * P:(k * 2 + part + 1) * P]

            def project_T(out, parts, c):
                cols = slice(c * CH, (c + 1) * CH)
                for k in range(KT):
                    for n, (a, b) in enumerate(three((0, xT_hi), (1, xT_hi), (0, xT_lo))):
                        last = nc.tensor.matmul(out, parts(a, k), b[:, k, cols],
                                                start=(k == 0 and n == 0), stop=(k == KT - 1 and n == 2))
                last.then_inc(unit_done, 1)

            def pair_units(first, c):
                for part in range(2):
                    pe.wait_ge(unit_free, first + part - 1)
                    project_T(unit_bank(part), lambda a, k: gu_slice((gu_hi, gu_lo)[a], k, part), c)

            def qk_units(first):
                for n in range(QK_UNITS):
                    pe.wait_ge(unit_free, first + n - 1)
                    project_T(unit_bank(n), lambda a, k: w_slice((qkv_hi, qkv_lo)[a], k, n // NC), n % NC)

            def out_units(first, products):
                for n in range(OUT_UNITS):
                    k, c = n // NC, n % NC
                    pe.wait_ge(unit_free, first + n - 1)
                    rows, cols = slice(k * P, (k + 1) * P), slice(c * CH, (c + 1) * CH)
                    todo = [(w, m) for blk, hi, lo in products
                            for w, m in three((ow_hi[:, blk, rows], hi(cols)), (ow_lo[:, blk, rows], hi(cols)),
                                              (ow_hi[:, blk, rows], lo(cols)))]
                    for q, (w, m) in enumerate(todo):
                        last = nc.tensor.matmul(unit_bank(n), w, m, start=(q == 0), stop=(q == len(todo) - 1))
                    last.then_inc(unit_done, 1)

            def hid_part(x_, b):
                return lambda cols: x_[:, b, cols]

            for a in range(2):
                half = a * (SHARED_UNITS // 2)
                for t in (2 * a, 2 * a + 1):
                    pe.wait_ge(gu_lo_done, t + 1)
                    for c in range(NC):
                        first = half + (t % 2) * 2 * NC + 2 * c
                        for part in range(2):
                            if first + part >= 2:
                                pe.wait_ge(unit_free, first + part - 1)
                            project_T(unit_bank(part), lambda q, k: gu_slice((gu_hi, gu_lo)[q], k, part), c)
                pe.wait_ge(hid_lo_done, (a + 1) * 2 * NC)
                pe.wait_ge(ow_lo_done, a + 1)
                out_units(half + 4 * NC, [(b, hid_part(hid_hi, b), hid_part(hid_lo, b)) for b in range(2)])
            pe.wait_ge(qkv_lo_done, 1)
            qk_units(SHARED_UNITS)

            def transposes(h, i):
                pe.wait_ge(normed, h.slot + i + 1)
                for tu in TU_OF[i]:
                    _, j, blocks = T_UNITS[tu]
                    if tu >= 2:
                        pe.wait_ge(pT_lo_done, h.tu + tu - 1)
                    for b in range(blocks):
                        last = nc.tensor.transpose(bank[:, T_BANK + tu % 2, b * P:(b + 1) * P],
                                                   probs[i % NP_][:, (j + b) * P:(j + b + 1) * P], ident[:])
                    last.then_inc(transposed, 1)

            def body(h, it):
                for n in range(V_UNITS):
                    pe.wait_ge(unit_free, h.v0 + n - 1)
                    for jj in range(TPC):
                        j = n * TPC + jj
                        rows = slice(j * P, (j + 1) * P)
                        for k in range(KT):
                            for q, (a, w) in enumerate(three((xT_hi, qkv_hi), (xT_lo, qkv_hi), (xT_hi, qkv_lo))):
                                last = nc.tensor.matmul(unit_bank(n)[:, jj * DV:(jj + 1) * DV], a[:, k, rows],
                                                        w_slice(w, k, 2), start=(k == 0 and q == 0),
                                                        stop=(k == KT - 1 and q == 2))
                    last.then_inc(unit_done, 1)
                pe.wait_ge(qk_lo_done, h.next_qk)
                for s in range(NT):
                    if s >= 2:
                        pe.wait_ge(exped, h.slot + s - 1)
                    for col, w in score_chunks(s):
                        out = bank[:, S_BANK + 2 * (s % 2) + col // CH, 0:w]
                        rows, cols = slice(s * P, (s + 1) * P), slice(col, col + w)
                        diagonal = col + w == (s + 1) * P
                        for n, (a, b) in enumerate(three((qk_hi, qk_hi), (qk_lo, qk_hi), (qk_hi, qk_lo))):
                            last = nc.tensor.matmul(out, a["q"][:, rows], b["k"][:, cols], start=(n == 0),
                                                    stop=(n == 2 and not diagonal))
                        if diagonal:
                            last = nc.tensor.matmul(out[:, w - P:w], ident_bf[:], mask_bf[:], start=False, stop=True)
                    last.then_inc(scored, 1)
                    if s >= LAG:
                        transposes(h, s - LAG)
                    if s in PAIR_SLOTS:
                        n = PAIR_SLOTS.index(s)
                        tile, c = PAIRS[h.hh][n]
                        if c == 0:
                            pe.wait_ge(gu_lo_done, h.tile + ST + tile + 1)
                        pair_units(h.pairs0 + 2 * n, c)
                if not h.last_head:
                    pe.wait_ge(qkv_lo_done, h.h + 2)
                    qk_units(h.next_qk0)
                for i in range(NT - LAG, NT):
                    transposes(h, i)
                for c in range(PV_UNITS):
                    pe.wait_ge(unit_free, h.pv0 + c - 1)
                    pe.wait_ge(pT_lo_done, h.tu + (TU_OF[TPC * (c + 1) - 1][-1] + 1))
                    pieces = pv_pieces(c)
                    for j, q in pieces:
                        for n, (a, b) in enumerate(three((v_hi, pT_hi), (v_lo, pT_hi), (v_hi, pT_lo))):
                            last = nc.tensor.matmul(unit_bank(c)[:, q:CH], a[:, j, :], b[c][:, j, q:CH],
                                                    start=(j == 0 and n == 0),
                                                    stop=(j == len(pieces) - 1 and n == 2))
                    last.then_inc(unit_done, 1)
                pe.wait_ge(unit_free, h.out0)
                pe.wait_ge(ow_lo_done, h.h + ST // 2 + 1)
                pe.wait_ge(hid_lo_done, h.pair + NPAIR)
                out_units(h.out0, [(0, lambda cols: head_hi[:, cols], lambda cols: head_lo[:, cols])] +
                          [(1 + b, hid_part(hid_hi, HID_BUF[t]), hid_part(hid_lo, HID_BUF[t]))
                           for b, t in enumerate(OUT_TILES[h.hh])])

            rounds(pe, body)


def _constants(np):
    f32 = np.float32
    t = np.arange(T, dtype=f32)
    theta = np.power(f32(10000.0), (f32(-2.0) * np.arange(HALF0, dtype=f32) / f32(DH0)).astype(f32)).astype(f32)
    ang = (t[:, None] * theta[None, :]).astype(f32)
    c0, s0 = (np.tile(f(ang.astype(np.float64)).astype(f32).T, (H0, 1)) for f in (np.cos, np.sin))
    half = DS // 2
    inv = (f32(1.0) / np.power(f32(10000.0), (np.arange(half, dtype=f32) / f32(half)).astype(f32)).astype(f32)).astype(f32)
    ang1 = (t[:, None] * inv[None, :]).astype(f32)
    c1, s1 = (f(ang1.astype(np.float64)).astype(f32).T for f in (np.cos, np.sin))
    one = np.ones((DS, T), f32)
    scale0 = f32(DH0 ** -0.5)
    mask = np.where(np.arange(P)[None, :] > np.arange(P)[:, None], f32(-1e30), f32(0.0)).astype(f32)
    return {
        "ident": np.eye(P, dtype=f32), "mask": mask,
        "cos_q": c0 * scale0, "sin_q": s0 * scale0, "cos_k": c0, "sin_k": s0,
        "cos1": np.concatenate([one, c1, c1]), "sin1": np.concatenate([one, -s1, s1]),
        "iota": np.tile(np.arange(NE, dtype=f32), (P, 1)),
    }


def _layout(np, a):
    def kp(w):
        return w.reshape(KT, P, -1).transpose(1, 0, 2)

    def rows(w):
        return w.reshape(-1, P, w.shape[-1]).transpose(1, 0, 2)

    even = [h * DH0 + 2 * i for h in range(H0) for i in range(HALF0)]
    odd = [n + 1 for n in even]
    wq, wk, wv = a["L0_attn_Wq"], a["L0_attn_Wk"], a["L0_attn_Wv"]
    out = {"x": a["L0_attn_X"][0]}
    out["w_qkv0"] = kp(np.concatenate([wq[even].T, wq[odd].T, wk[even].T, wk[odd].T, wv.T], axis=1))
    out["up0"] = kp(a["L0_ffn_up_weight"].T)
    out["down0"] = rows(a["L0_ffn_down_weight"].T)
    out["up_scale"] = a["L0_ffn_up_scale"].reshape(UT, P).T
    out["down_scale"] = np.tile(a["L0_ffn_down_scale"], (P, 1))
    out["out_scale"] = np.tile(a["L0_ffn_output_scale"], (P, 1))
    wo = np.zeros((H0, 2 * DH0, D), np.float32)
    wo[:, :DH0] = a["L0_attn_Wo"].T.reshape(H0, DH0, D)
    out["wo0"] = rows(wo.reshape(-1, D))
    pad = np.zeros((D, 1), np.float32)
    out["router"] = kp(np.concatenate([a["L1_ffn_gate_w"].T, a["L1_ffn_shared_expert_gate_w"].T, pad], axis=1))
    parts = []
    for h in range(H1):
        s = slice(h * DS, (h + 1) * DS)
        w = np.concatenate([a["L1_attn_wq_sem"][:, s], a["L1_attn_wq_geo"][:, s], a["L1_attn_wk_sem"][:, s],
                            a["L1_attn_wk_geo"][:, s], a["L1_attn_wv"][:, h * DV:(h + 1) * DV]], axis=1)
        parts.append(kp(w).reshape(P, -1))
    out["w_qkv1"] = np.stack(parts)
    out["gate_logit"] = np.tile(a["L1_attn_gate_logit"], (P, 1))
    rw = P // EG
    gu = a["L1_ffn_gate_up_proj"].reshape(NEG, EG, 2, ET, rw, KT, P)
    out["gu1"] = gu.transpose(0, 3, 6, 5, 2, 1, 4).reshape(NEG * ET, P, -1)
    dn = a["L1_ffn_down_proj"].reshape(NEG, EG, D, ET, rw).transpose(0, 3, 1, 4, 2).reshape(NEG, ET, P, D)
    wo1 = a["L1_attn_wo"].reshape(NEG, HPI, DV, D)
    out["ow_a"] = np.stack([wo1[:, 0], dn[:, 0]], axis=2)
    out["ow_b"] = np.stack([wo1[:, 1], dn[:, 1], dn[:, 2]], axis=2)
    sg = np.stack([a["L1_ffn_shared_gate_w"], a["L1_ffn_shared_up_w"]])
    out["gu_shared"] = sg.reshape(2, ST, P, KT, P).transpose(1, 4, 3, 0, 2).reshape(ST, P, -1)
    out["down_shared"] = a["L1_ffn_shared_down_w"].T.reshape(ST // 2, 2, P, D).transpose(0, 2, 1, 3)
    return out


def kernel(**inputs):
    import numpy as _np
    import concourse.bacc as _bacc
    from concourse import mybir as _mybir
    from concourse.bass_utils import run_bass_kernel_spmd as _run

    nc = _bacc.Bacc("TRN2", target_bir_lowering=False, num_devices=1)
    host = _layout(_np, {k: _np.asarray(v) for k, v in inputs.items()})
    host.update(_constants(_np))
    arrays, tensors = {}, {}
    for name, value in host.items():
        value = _np.ascontiguousarray(value)
        arrays[f"in_{name}"] = value
        tensors[name] = nc.dram_tensor(f"in_{name}", value.shape, _mybir.dt.from_np(value.dtype),
                                       kind="ExternalInput").ap()
    tensors["out"] = nc.dram_tensor("outT", (KT, P, T), _mybir.dt.float32, kind="ExternalOutput").ap()
    build(nc, tensors)
    r = _run(nc, [arrays], core_ids=[0])
    return r.results[0]["outT"].reshape(D, T).T.reshape(1, T, D)
```

```python
from contextlib import ExitStack

import concourse.bass as bass
from concourse import mybir

F32 = mybir.dt.float32
F32R = mybir.dt.float32r
BF16 = mybir.dt.bfloat16
U32 = mybir.dt.uint32
ALU = mybir.AluOpType
ACT = mybir.ActivationFunctionType
AX_X = mybir.AxisListType.X

P = 128
T = 1024
D = 256
KT = D // P
NT = T // P
CH = 512
NC = T // CH
TPC = CH // P
EPS = 1e-5

H0 = 16
DH0 = D // H0
HALF0 = DH0 // 2
GH = 4
NG = H0 // GH
HID = 1024
UT = HID // P
STACK = 4 * DH0

H1 = 16
DS = 64
DV = 128
NE = 32
TOPK = 4
DMOE = 96
EG = 4
ET = EG * DMOE // P
NEG = NE // EG
SH = 512
ST = SH // P
HPI = H1 // NEG
assert HPI == 2 and ET == 3

T_UNITS = [(i, j, min(4, i + 1 - j)) for i in range(NT) for j in range(0, i + 1, 4)]
NTU = len(T_UNITS)
TU_OF = [[n for n, u in enumerate(T_UNITS) if u[0] == i] for i in range(NT)]


def score_chunks(i):
    width = (i + 1) * P
    return [(c, min(CH, width - c)) for c in range(0, width, CH)]


def pv_pieces(c):
    return [(j, max(0, j * P - c * CH)) for j in range((c + 1) * TPC)]


def three(hi_hi, lo_hi, hi_lo):
    return (hi_hi, lo_hi, hi_lo)


class Semaphores:
    def __init__(self, nc, ctx, prefix):
        self.nc, self.ctx, self.prefix = nc, ctx, prefix

    def __call__(self, name):
        return self.ctx.enter_context(self.nc.semaphore(self.prefix + name))


def build(nc, d):
    with ExitStack() as ctx:
        def sb(name, shape, dt=F32, on=ctx):
            return on.enter_context(nc.sbuf_tensor(name, shape, dt))

        ident = sb("ident", [P, P])
        ident_bf = sb("ident_bf", [P, P], BF16)
        mask_bf = sb("mask_bf", [P, P], BF16)
        xT_hi, xT_lo = sb("xT_hi", [P, KT, T], F32R), sb("xT_lo", [P, KT, T], F32R)
        acc = sb("acc", [P, KT, T])
        bank = ctx.enter_context(nc.psum_tensor("bank", [P, 8, CH], F32))
        rope_scratch = {
            n: nc.dram_tensor(f"{n}_stack", (H0, STACK, T), F32, kind="Internal").ap() for n in "qk"}
        comb_scratch = nc.dram_tensor("comb_scratch", (NE + 1, T), F32, kind="Internal").ap()

        with ExitStack() as layer0:
            x = sb("x", [P, NT, D], on=layer0)
            v_sb = sb("v_sb", [P, NT, D], on=layer0)
            with ExitStack() as a:
                project_layer0(nc, d, a, sb, bank, x, acc, xT_hi, xT_lo, ident, ident_bf, mask_bf, v_sb, rope_scratch)
            heads_hi = sb("heads_hi", [P, NG, T], F32R, on=layer0)
            heads_lo = sb("heads_lo", [P, NG, T], F32R, on=layer0)
            with ExitStack() as b:
                attend_layer0(nc, d, b, sb, bank, ident, ident_bf, mask_bf, v_sb, rope_scratch,
                              heads_hi, heads_lo,
                              *([w[:, n, :] for n in range(2)] for w in (xT_hi, xT_lo, acc)))
            with ExitStack() as c:
                join_layer0(nc, d, c, sb, bank, x, ident, heads_hi, heads_lo, xT_hi, xT_lo, acc,
                            comb_scratch)
        with ExitStack() as e:
            layer1(nc, d, e, sb, bank, ident, ident_bf, mask_bf, xT_hi, xT_lo, acc, comb_scratch)


class Norm:

    def __init__(self, nc, sb, on, prefix):
        self.nc = nc
        self.stats = sb(prefix + "stats", [P, NT, 6], on=on)
        self.mv = sb(prefix + "mv", [P, NT, 2], on=on)
        self.var = sb(prefix + "var", [P, NT], on=on)
        self.sd = sb(prefix + "sd", [P, NT], on=on)
        self.r0 = sb(prefix + "r0", [P, NT], on=on)
        self.r1 = sb(prefix + "r1", [P, NT], on=on)
        self.r2 = sb(prefix + "r2", [P, NT], on=on)
        self.r3 = sb(prefix + "r3", [P, NT], on=on)
        self.rstd = sb(prefix + "rstd", [P, NT], on=on)
        self.step = on.enter_context(nc.semaphore(prefix + "norm_step"))
        self.sqrt = on.enter_context(nc.semaphore(prefix + "norm_sqrt"))

    VAR_STEP = 2 * NT + 1

    def on_vector(self, dve, src, out):
        nc, n = self.nc, 0
        for j in range(NT):
            nc.vector.bn_stats(self.stats[:, j, :], src[:, j, :]).then_inc(self.step, 1)
        for j in range(NT):
            dve.wait_ge(self.step, NT)
            nc.vector.bn_aggr(self.mv[:, j, :], self.stats[:, j, :]).then_inc(self.step, 1)
        dve.wait_ge(self.step, 2 * NT)
        nc.vector.tensor_scalar(self.var[:], self.mv[:, :, 1], EPS, None, ALU.add).then_inc(self.step, 1)
        n = self.VAR_STEP
        dve.wait_ge(self.sqrt, 1)
        nc.vector.reciprocal(self.r0[:], self.sd[:]).then_inc(self.step, 1)
        dve.wait_ge(self.step, n + 1)
        nc.vector.tensor_tensor(self.r1[:], self.r0[:], self.r0[:], ALU.mult).then_inc(self.step, 1)
        dve.wait_ge(self.step, n + 2)
        nc.vector.tensor_tensor(self.r2[:], self.r1[:], self.var[:], ALU.mult).then_inc(self.step, 1)
        dve.wait_ge(self.step, n + 3)
        nc.vector.tensor_scalar(self.r3[:], self.r2[:], -0.5, 1.5, ALU.mult, ALU.add).then_inc(self.step, 1)
        dve.wait_ge(self.step, n + 4)
        nc.vector.tensor_tensor(self.rstd[:], self.r0[:], self.r3[:], ALU.mult).then_inc(self.step, 1)
        dve.wait_ge(self.step, n + 5)
        for j in range(NT):
            nc.vector.tensor_scalar(out[:, j, :], src[:, j, :], self.mv[:, j, 0:1], self.rstd[:, j:j + 1],
                                    ALU.subtract, ALU.mult).then_inc(self.step, 1)

    DONE = VAR_STEP + 5

    def on_scalar(self, act):
        act.wait_ge(self.step, self.VAR_STEP)
        self.nc.scalar.activation(self.sd[:], self.var[:], ACT.Sqrt).then_inc(self.sqrt, 1)


def project_layer0(nc, d, ctx, sb, bank, x, room, xT_hi, xT_lo, ident, ident_bf, mask_bf, v_sb, rope_scratch):
    sem = Semaphores(nc, ctx, "a_")

    def buf(name, shape, dt=F32):
        return sb("a_" + name, shape, dt, on=ctx)

    mask = buf("mask", [P, P])
    xn = room[:].rearrange("p k t -> p (k t)").rearrange("p (j d) -> p j d", j=NT)
    w = buf("w", [P, KT, 3 * D])
    w_hi, w_lo = buf("w_hi", [P, KT, 3 * D], F32R), buf("w_lo", [P, KT, 3 * D], F32R)
    table = {n: buf(n, [P, T]) for n in ("cos_q", "sin_q", "cos_k", "sin_k")}
    prod = [buf(f"prod{n}", [P, T]) for n in range(3)]
    rot = [buf(f"rot{n}", [P, T]) for n in range(1)]
    part_hi = [buf(f"part_hi{m}", [P, T], F32R) for m in range(4)]
    part_lo = [buf(f"part_lo{m}", [P, T], F32R) for m in range(4)]
    up = buf("up", [P, KT, HID])
    up_sign = buf("up_sign", [P, KT, HID], F32R)
    down = buf("down", [P, UT, D])
    down_sign = buf("down_sign", [P, UT, D], F32R)
    up_scale, down_scale, out_scale = buf("ups", [P, UT]), buf("downs", [P, D]), buf("outs", [P, 1])
    hid = [buf(f"hid{n}", [P, CH]) for n in range(2)]
    hid_hi, hid_lo = buf("hid_hi", [P, UT, CH], F32R), buf("hid_lo", [P, UT, CH], F32R)
    scaled = [buf(f"scaled{n}", [P, D]) for n in range(2)]
    norm = Norm(nc, sb, ctx, "a_")

    x_in, const_in, w_in, table_in, ffn_in = sem("x_in"), sem("const_in"), sem("w_in"), sem("table_in"), sem("ffn_in")
    consts = sem("consts")
    w_hi_done, w_lo_done, signs_done = sem("w_hi_done"), sem("w_lo_done"), sem("signs_done")
    transposed, xT_hi_done, xT_lo_done = sem("transposed"), sem("xT_hi_done"), sem("xT_lo_done")
    projected = sem("projected")
    rope_step = sem("rope_step")
    rot_hi_done = sem("rot_hi_done")
    v_projected, v_copied = sem("v_projected"), sem("v_copied")
    up_done, relu_done, hid_hi_done, hid_lo_done = sem("up_done"), sem("relu_done"), sem("hid_hi_done"), sem("hid_lo_done")
    down_done, down_scaled, x_added = sem("down_done"), sem("down_scaled"), sem("x_added")
    stored = sem("stored")

    STEPS = 4
    NU = NC * UT

    with nc.Block() as block:
        @block.sync
        def _(sp):
            sp.dma_start(x[:], d["x"].rearrange("(j p) d -> p j d", p=P)).then_inc(x_in, 16)
            sp.dma_start(ident[:], d["ident"]).then_inc(const_in, 16)
            sp.dma_start(mask[:], d["mask"]).then_inc(const_in, 16)
            sp.dma_start(w[:], d["w_qkv0"]).then_inc(w_in, 16)
            for n in table:
                sp.dma_start(table[n][:], d[n]).then_inc(table_in, 16)
            sp.dma_start(up[:], d["up0"]).then_inc(ffn_in, 16)
            sp.dma_start(down[:], d["down0"]).then_inc(ffn_in, 16)
            sp.dma_start(up_scale[:], d["up_scale"]).then_inc(ffn_in, 16)
            sp.dma_start(down_scale[:], d["down_scale"]).then_inc(ffn_in, 16)
            sp.dma_start(out_scale[:], d["out_scale"]).then_inc(ffn_in, 16)
            for m in range(4):
                which, half = "qk"[m // 2], m % 2
                sp.wait_ge(rope_step, STEPS * (m + 1))
                for rep in range(2):
                    for part, src in enumerate((part_hi[m], part_lo[m])):
                        row = (rep * 2 + part if which == "q" else part * 2 + rep) * DH0 + half * HALF0
                        sp.dma_start(rope_scratch[which][:, row:row + HALF0, :], src[:].bitcast(F32)).then_inc(stored, 16)
            sp.wait_ge(stored, 16 * 16)

        @block.scalar
        def _(act):
            act.wait_ge(w_in, 16)
            nc.scalar.copy(w_hi[:], w[:]).then_inc(w_hi_done, 1)
            norm.on_scalar(act)
            for c in range(KT):
                for n in range(NC):
                    act.wait_ge(transposed, c * NC + n + 1)
                    nc.scalar.copy(xT_hi[:, c, n * CH:(n + 1) * CH], bank[:, c * NC + n, :]).then_inc(xT_hi_done, 1)
            act.wait_ge(ffn_in, 80)
            nc.scalar.activation(up_sign[:], up[:], ACT.Sign).then_inc(signs_done, 1)
            nc.scalar.activation(down_sign[:], down[:], ACT.Sign).then_inc(signs_done, 1)
            for m in range(4):
                act.wait_ge(rope_step, STEPS * m + 3)
                nc.scalar.copy(part_hi[m][:], rot[0][:]).then_inc(rot_hi_done, 1)
            for n in range(NT // 2):
                act.wait_ge(v_projected, n + 1)
                nc.scalar.copy(v_sb[:, 2 * n:2 * n + 2, :],
                               bank[:, 4 + n, :].rearrange("p (j d) -> p j d", j=2)).then_inc(v_copied, 1)
            for n in range(NU):
                act.wait_ge(up_done, n + 1)
                if n >= 2:
                    act.wait_ge(hid_lo_done, n - 1)
                nc.scalar.activation(hid[n % 2][:], bank[:, n % 4, :], ACT.Relu,
                                     scale=up_scale[:, n % UT:n % UT + 1]).then_inc(relu_done, 1)

        @block.vector
        def _(dve):
            dve.wait_ge(x_in, 16)
            norm.on_vector(dve, x, xn)
            dve.wait_ge(const_in, 32)
            nc.vector.tensor_copy(ident_bf[:], ident[:]).then_inc(consts, 1)
            nc.vector.tensor_copy(mask_bf[:], mask[:]).then_inc(consts, 1)
            dve.wait_ge(w_hi_done, 1)
            nc.vector.tensor_tensor(w_lo[:], w[:], w_hi[:].bitcast(F32), ALU.subtract).then_inc(w_lo_done, 1)
            for c in range(KT):
                for n in range(NC):
                    dve.wait_ge(xT_hi_done, c * NC + n + 1)
                    cols = slice(n * CH, (n + 1) * CH)
                    nc.vector.tensor_tensor(xT_lo[:, c, cols], bank[:, c * NC + n, :],
                                            xT_hi[:, c, cols].bitcast(F32), ALU.subtract).then_inc(xT_lo_done, 1)
            dve.wait_ge(table_in, 64)
            done = 0
            for m in range(4):
                which, half = "qk"[m // 2], m % 2
                base = 4 if which == "q" else 0
                even = bank[:, base:base + 2, :].rearrange("p b t -> p (b t)")
                odd = bank[:, base + 2:base + 4, :].rearrange("p b t -> p (b t)")
                cos, sin = table["cos_" + which], table["sin_" + which]
                dve.wait_ge(projected, 4 * (m // 2) + 4)
                if m >= 1:
                    dve.wait_ge(rope_step, done)
                nc.vector.tensor_tensor(prod[0][:], even, (cos if half == 0 else sin)[:], ALU.mult).then_inc(rope_step, 1)
                nc.vector.tensor_tensor(prod[1][:], odd, (sin if half == 0 else cos)[:], ALU.mult).then_inc(rope_step, 1)
                dve.wait_ge(rope_step, done + 2)
                nc.vector.tensor_tensor(rot[0][:], prod[0][:], prod[1][:],
                                        ALU.subtract if half == 0 else ALU.add).then_inc(rope_step, 1)
                dve.wait_ge(rope_step, done + 3)
                dve.wait_ge(rot_hi_done, m + 1)
                nc.vector.tensor_tensor(part_lo[m][:], rot[0][:], part_hi[m][:].bitcast(F32),
                                        ALU.subtract).then_inc(rope_step, 1)
                done += STEPS

            def down_units(c):
                for n in range(c * TPC, (c + 1) * TPC):
                    dve.wait_ge(down_done, n + 1)
                    if n >= 2:
                        dve.wait_ge(x_added, n - 1)
                    nc.vector.tensor_tensor(scaled[n % 2][:], bank[:, 4 + n % 4, 0:D], down_scale[:],
                                            ALU.mult).then_inc(down_scaled, 1)
                    dve.wait_ge(down_scaled, n + 1)
                    nc.vector.scalar_tensor_tensor(x[:, n, :], scaled[n % 2][:], out_scale[:, 0:1], x[:, n, :],
                                                   ALU.mult, ALU.add).then_inc(x_added, 1)

            for c in range(NC):
                for u in range(UT):
                    n = c * UT + u
                    dve.wait_ge(relu_done, n + 1)
                    if c:
                        dve.wait_ge(down_done, c * TPC)
                    nc.vector.tensor_copy(hid_hi[:, u, :], hid[n % 2][:]).then_inc(hid_hi_done, 1)
                down_units(c)

        @block.gpsimd
        def _(pool):
            for n in range(NU):
                pool.wait_ge(hid_hi_done, n + 1)
                nc.gpsimd.tensor_tensor(hid_lo[:, n % UT, :], hid[n % 2][:],
                                        hid_hi[:, n % UT, :].bitcast(F32), ALU.subtract).then_inc(hid_lo_done, 1)

        @block.tensor
        def _(pe):
            pe.wait_ge(const_in, 32)
            for c in range(KT):
                for j in range(NT):
                    pe.wait_ge(norm.step, norm.DONE + (j + 1 if c == 0 else NT))
                    last = nc.tensor.transpose(bank[:, c * NC + j // TPC, (j % TPC) * P:(j % TPC + 1) * P],
                                               xn[:, j, c * P:(c + 1) * P], ident[:])
                    if j % TPC == TPC - 1:
                        last.then_inc(transposed, 1)
            pe.wait_ge(w_lo_done, 1)
            pe.wait_ge(xT_lo_done, KT * NC)
            for m in range(4):
                for c in range(NC):
                    out = bank[:, (4 + 2 * m + c) % 8, :]
                    cols = slice(c * CH, (c + 1) * CH)
                    for k in range(KT):
                        for n, (a, b) in enumerate(three((w_hi, xT_hi), (w_lo, xT_hi), (w_hi, xT_lo))):
                            last = nc.tensor.matmul(out, a[:, k, m * P:(m + 1) * P], b[:, k, cols],
                                                    start=(k == 0 and n == 0), stop=(k == KT - 1 and n == 2))
                    last.then_inc(projected, 1)
            for jj in range(NT // 2):
                pe.wait_ge(rope_step, 2 * STEPS)
                for j in (2 * jj, 2 * jj + 1):
                    out = bank[:, 4 + jj, (j % 2) * D:(j % 2 + 1) * D]
                    rows = slice(j * P, (j + 1) * P)
                    for k in range(KT):
                        for n, (a, b) in enumerate(three((xT_hi, w_hi), (xT_lo, w_hi), (xT_hi, w_lo))):
                            last = nc.tensor.matmul(out, a[:, k, rows], b[:, k, 2 * D:3 * D],
                                                    start=(k == 0 and n == 0), stop=(k == KT - 1 and n == 2))
                last.then_inc(v_projected, 1)
            pe.wait_ge(signs_done, 2)
            pe.wait_ge(rope_step, 4 * STEPS)
            pe.wait_ge(v_copied, NT // 2)
            for c in range(NC):
                for u in range(UT):
                    n = c * UT + u
                    if n >= 4:
                        pe.wait_ge(relu_done, n - 3)
                    for k in range(KT):
                        for q, b in enumerate((xT_hi, xT_lo)):
                            last = nc.tensor.matmul(bank[:, n % 4, :], up_sign[:, k, u * P:(u + 1) * P],
                                                    b[:, k, c * CH:(c + 1) * CH],
                                                    start=(k == 0 and q == 0), stop=(k == KT - 1 and q == 1))
                    last.then_inc(up_done, 1)
                for j in range(TPC):
                    n = c * TPC + j
                    pe.wait_ge(hid_lo_done, (c + 1) * UT)
                    if n >= 4:
                        pe.wait_ge(down_scaled, n - 3)
                    for u in range(UT):
                        for q, a in enumerate((hid_hi, hid_lo)):
                            last = nc.tensor.matmul(bank[:, 4 + n % 4, 0:D], a[:, u, j * P:(j + 1) * P],
                                                    down_sign[:, u, :], start=(u == 0 and q == 0),
                                                    stop=(u == UT - 1 and q == 1))
                    last.then_inc(down_done, 1)


def attend_layer0(nc, d, ctx, sb, bank, ident, ident_bf, mask_bf, v_sb, rope_scratch, heads_hi, heads_lo, q_pair, k_pair,
                  room):
    sem = Semaphores(nc, ctx, "b_")

    def buf(name, shape, dt=F32):
        return sb("b_" + name, shape, dt, on=ctx)

    SLOTS = GH * NT
    TUS = GH * NTU
    PRE = 6
    probs = room + [buf(f"probs{n}", [P, T]) for n in range(8 - len(room))]
    NP_ = len(probs)
    assert SLOTS % NP_ == 0 and PRE <= NP_
    neg_max, row_sum, row_inv = buf("neg_max", [P, SLOTS]), buf("row_sum", [P, SLOTS]), buf("row_inv", [P, SLOTS])
    probsT = [[buf(f"probsT{h}_{c}", [P, (c + 1) * TPC, CH]) for c in range(NC)] for h in range(GH)]
    v_group = buf("v_group", [P, NT, GH, 2 * DH0])

    pair_in = [sem(f"pair_in{n}") for n in range(2)]
    scored, maxed, exped, inverted, normed = sem("scored"), sem("maxed"), sem("exped"), sem("inverted"), sem("normed")
    transposed = sem("transposed")
    copied = [sem("copied_by_act"), sem("copied_by_dve")]
    v_cleared, v_ready, inverted_seen = sem("v_cleared"), sem("v_ready"), sem("inverted_seen")
    mixed, heads_hi_done, heads_lo_done = sem("mixed"), sem("heads_hi_done"), sem("heads_lo_done")

    stack = {n: rope_scratch[n].rearrange("(pair two) r t -> pair (two r) t", two=2) for n in "qk"}
    S_BANK, T_BANK, O_BANK = 0, 4, 7
    T_RING = 3
    assert NTU % T_RING == 0
    COPIER = [0, 0, 0, 1, 1, 0, 1, 0, 1, 0, 1, 0]
    COPIES = [COPIER.count(e) for e in range(2)]
    NTH = [COPIER[:tu].count(COPIER[tu]) for tu in range(NTU)]

    T_LAG = 4.25
    MIX_AT = [SLOTS - 1 - TPC + T_LAG + 1.6, SLOTS - 1 + T_LAG + 2.1]

    def steps(last, *kinds):
        out = []
        for name, lag, first, count in kinds:
            for n in range(first, first + count):
                if not (last and n >= SLOTS):
                    out.append(((MIX_AT[n] if name == "mix" else n) + lag, name, n))
        return [(name, n) for _, name, n in sorted(out, key=lambda step: step[0])]

    def rounds(engine, body):
        with engine.Fori(0, NG - 1) as g:
            body(g, False)
        body(NG - 1, True)

    def width(s):
        return (s % NT + 1) * P

    def score_bank(s):
        return bank[:, S_BANK + 2 * (s % 2):S_BANK + 2 * (s % 2) + 2, :].rearrange("p b t -> p (b t)")[:, 0:width(s)]

    def col(s):
        return slice(s % SLOTS, s % SLOTS + 1)

    def unit(s, tu):
        return s // NT * NTU + tu

    with nc.Block() as block:
        @block.sync
        def _(sp):
            def load(g, pr):
                src = {n: stack[n].rearrange("(g two) p t -> g two p t", two=2)[bass.ds(g, 1), pr, :, :]
                       .rearrange("g p t -> (g p) t") for n in "qk"}
                sp.dma_start(q_pair[pr][:].bitcast(F32), src["q"]).then_inc(pair_in[pr], 16)
                sp.dma_start(k_pair[pr][:].bitcast(F32), src["k"]).then_inc(pair_in[pr], 16)

            for pr in range(2):
                load(0, pr)
            with sp.Fori(0, NG - 1) as g:
                for pr in range(2):
                    sp.wait_ge(scored, g * SLOTS + (pr + 1) * (SLOTS // 2))
                    load(g + 1, pr)

        @block.gpsimd
        def _(pool):
            def normalise(g, s):
                pool.wait_ge(inverted, g * SLOTS + s + 1)
                pool.sem_inc(inverted_seen)
                nc.gpsimd.tensor_scalar(probs[s % NP_][:, 0:width(s)], probs[s % NP_][:, 0:width(s)],
                                        row_inv[:, col(s)], 1.0, ALU.mult, ALU.mult).then_inc(normed, 1)

            nc.gpsimd.memset(v_group[:], 0.0).then_inc(v_cleared, 1)
            for s in range(PRE):
                normalise(0, s)

            def body(g, last):
                for name, n in steps(last, ("norm", 0, PRE, SLOTS), ("values", PRE + 2, 0, 1)):
                    if name == "norm":
                        normalise(g, n)
                    else:
                        pool.wait_ge(v_cleared, 1)
                        pool.wait_ge(heads_lo_done, g * NC + 1)
                        src = v_sb[:].rearrange("p j (g h e) -> p j g h e", g=NG, h=GH)[:, :, bass.ds(g, 1), :, :]
                        nc.gpsimd.tensor_copy(v_group[:, :, :, 0:DH0], src.rearrange("p j g h e -> p j (g h) e")
                                              ).then_inc(v_ready, 1)

            rounds(pool, body)

        def evacuate(eng, copy, g, s, mine):
            i = s % NT
            for tu in TU_OF[i]:
                if COPIER[tu] != mine:
                    continue
                _, j, blocks = T_UNITS[tu]
                eng.wait_ge(transposed, g * TUS + unit(s, tu) + 1)
                c, at = i // TPC, (i % TPC) * P
                copy(probsT[s // NT][c][:, j:j + blocks, at:at + P],
                     bank[:, T_BANK + tu % T_RING, 0:blocks * P].rearrange("p (b q) -> p b q", b=blocks)
                     ).then_inc(copied[mine], 1)

        @block.scalar
        def _(act):
            def exp(g, s):
                act.wait_ge(maxed, g * SLOTS + s + 1)
                nc.scalar.activation(probs[s % NP_][:, 0:width(s)], score_bank(s), ACT.Exp, bias=neg_max[:, col(s)],
                                     accum_out=row_sum[:, col(s)]).then_inc(exped, 1)

            for s in range(PRE):
                exp(0, s)

            def body(g, last):
                for name, n in steps(last, ("exp", 0, PRE, SLOTS), ("copy", T_LAG + 0.4, 0, SLOTS), ("mix", 0.5, 0, NC)):
                    if name == "exp":
                        if n >= NP_:
                            act.wait_ge(transposed, g * TUS + unit(n - NP_, TU_OF[(n - NP_) % NT][-1]) + 1)
                        exp(g, n)
                    elif name == "copy":
                        evacuate(act, nc.scalar.copy, g, n, 0)
                    else:
                        act.wait_ge(mixed, g * NC + n + 1)
                        out = heads_hi[:, bass.ds(g, 1), n * CH:(n + 1) * CH].rearrange("p g t -> p (g t)")
                        nc.scalar.copy(out, bank[:, O_BANK, :]).then_inc(heads_hi_done, 1)

            rounds(act, body)

        @block.vector
        def _(dve):
            dve.sem_inc(heads_lo_done)
            dve.sem_inc(copied[0], COPIES[0])
            dve.sem_inc(copied[1], COPIES[1])

            def maximum(g, s):
                dve.wait_ge(scored, g * SLOTS + s + 1)
                nc.vector.tensor_reduce(neg_max[:, col(s)], score_bank(s), AX_X, ALU.max, negate=True).then_inc(maxed, 1)

            def inverse(g, s):
                dve.wait_ge(exped, g * SLOTS + s + 1)
                nc.vector.reciprocal(row_inv[:, col(s)], row_sum[:, col(s)]).then_inc(inverted, 1)

            for s in range(PRE):
                maximum(0, s)
                if s >= 2:
                    inverse(0, s - 2)
            for s in range(PRE - 2, PRE):
                inverse(0, s)

            def body(g, last):
                for name, n in steps(last, ("max", 0, PRE, SLOTS), ("inv", 2.1, PRE, SLOTS),
                                     ("copy", T_LAG - 0.1, 0, SLOTS), ("mix", 2.5, 0, NC)):
                    if name == "max":
                        maximum(g, n)
                    elif name == "inv":
                        inverse(g, n)
                    elif name == "copy":
                        evacuate(dve, nc.vector.tensor_copy, g, n, 1)
                    else:
                        dve.wait_ge(heads_hi_done, g * NC + n + 1)
                        cols = slice(n * CH, (n + 1) * CH)
                        nc.vector.tensor_tensor(
                            heads_lo[:, bass.ds(g, 1), cols].rearrange("p g t -> p (g t)"), bank[:, O_BANK, :],
                            heads_hi[:, bass.ds(g, 1), cols].rearrange("p g t -> p (g t)").bitcast(F32),
                            ALU.subtract).then_inc(heads_lo_done, 1)

            rounds(dve, body)

        @block.tensor
        def _(pe):
            def scores(g, s):
                h, i = s % SLOTS // NT, s % NT
                rows = slice((h % 2) * STACK, (h % 2 + 1) * STACK)
                if i == 0 and h % 2 == 0:
                    pe.wait_ge(pair_in[h // 2], (g + s // SLOTS) * 32 + 32)
                for at, w in score_chunks(i):
                    out = bank[:, S_BANK + 2 * (s % 2) + at // CH, 0:w]
                    diagonal = at + w == (i + 1) * P
                    last = nc.tensor.matmul(out, q_pair[h // 2][rows, i * P:(i + 1) * P],
                                            k_pair[h // 2][rows, at:at + w], start=True, stop=not diagonal)
                    if diagonal:
                        last = nc.tensor.matmul(out[:, w - P:w], ident_bf[:], mask_bf[:], start=False, stop=True)
                last.then_inc(scored, 1)

            for s in range(PRE):
                if s >= 2:
                    pe.wait_ge(exped, s - 1)
                scores(0, s)
            pe.wait_ge(copied[1], COPIES[1])

            def body(g, last):
                for name, n in steps(last, ("score", 0, PRE, SLOTS), ("transpose", T_LAG, 0, SLOTS), ("mix", 0, 0, NC)):
                    if name == "score":
                        pe.wait_ge(exped, g * SLOTS + n - 1)
                        scores(g, n)
                    elif name == "transpose":
                        pe.wait_ge(normed, g * SLOTS + n + 1)
                        for tu in TU_OF[n % NT]:
                            back = (tu - T_RING) % NTU
                            head = n // NT + (0 if tu >= T_RING else -1)
                            e = COPIER[back]
                            pe.wait_ge(copied[e], g * (GH * COPIES[e]) + (head + 1) * COPIES[e] + NTH[back] + 1)
                            _, j, blocks = T_UNITS[tu]
                            for b in range(blocks):
                                last_ = nc.tensor.transpose(bank[:, T_BANK + tu % T_RING, b * P:(b + 1) * P],
                                                            probs[n % NP_][:, (j + b) * P:(j + b + 1) * P], ident[:])
                            last_.then_inc(transposed, 1)
                    else:
                        pe.wait_ge(v_ready, g + 1)
                        pe.wait_ge(heads_lo_done, g * NC + n + 1)
                        for e in range(2):
                            units = [u for u in TU_OF[TPC * (n + 1) - 2] + TU_OF[TPC * (n + 1) - 1] if COPIER[u] == e]
                            pe.wait_ge(copied[e], g * (GH * COPIES[e]) + GH * COPIES[e] + NTH[units[-1]] + 1)
                        pieces = pv_pieces(n)
                        for j, q in pieces:
                            for h in range(GH):
                                last_ = nc.tensor.matmul(bank[32 * h:32 * h + 32, O_BANK, q:CH],
                                                         v_group[:, j, h, :], probsT[h][n][:, j, q:CH],
                                                         start=(j == 0), stop=(j == len(pieces) - 1))
                        last_.then_inc(mixed, 1)

            rounds(pe, body)


def join_layer0(nc, d, ctx, sb, bank, x, ident, heads_hi, heads_lo, xT_hi, xT_lo, acc, comb_scratch):
    sem = Semaphores(nc, ctx, "c_")

    def buf(name, shape, dt=F32):
        return sb("c_" + name, shape, dt, on=ctx)

    NR = NE + 2
    wo = buf("wo", [P, NG, D])
    wo_hi, wo_lo = buf("wo_hi", [P, NG, D], F32R), buf("wo_lo", [P, NG, D], F32R)
    wr = buf("wr", [P, KT, NR])
    wr_hi, wr_lo = buf("wr_hi", [P, KT, NR], F32R), buf("wr_lo", [P, KT, NR], F32R)
    iota = buf("iota", [P, NE])
    xn = buf("xn", [P, NT, D])
    norm = Norm(nc, sb, ctx, "c_")
    logits = buf("logits", [P, NT, NR])
    row = {n: buf(n, [P, NT, 1]) for n in ("mx", "sum", "inv", "sum4", "sum4e", "inv4", "ez", "ez1", "gate")}
    shifted, expd, soft, hit, hitw = (buf(n, [P, NT, NE]) for n in ("shifted", "expd", "soft", "hit", "hitw"))
    top, top_id = buf("top", [P, NT, 8]), buf("top_id", [P, NT, 8], U32)
    top_idf, top_w = buf("top_idf", [P, NT, 8]), buf("top_w", [P, NT, 8])
    comb = buf("comb", [P, NT, 64])
    combT = buf("combT", [64, T])

    w_in, w_hi_done, w_lo_done = sem("w_in"), sem("w_hi_done"), sem("w_lo_done")
    projected, joined = sem("projected"), sem("joined")
    x_transposed, acc_done, n_transposed, xT_hi_done, xT_lo_done = (
        sem("x_transposed"), sem("acc_done"), sem("n_transposed"), sem("xT_hi_done"), sem("xT_lo_done"))
    routed, logits_out, step, exps = sem("routed"), sem("logits_out"), sem("step"), sem("exps")
    comb_transposed, combT_done, stored = sem("comb_transposed"), sem("combT_done"), sem("stored")
    SHIFT_STEP = 2
    ROUTE_STEPS = SHIFT_STEP + 3 + 2 * NT + 6 + 3 * TOPK + 3

    with nc.Block() as block:
        @block.sync
        def _(sp):
            sp.dma_start(wo[:], d["wo0"]).then_inc(w_in, 16)
            sp.dma_start(wr[:], d["router"]).then_inc(w_in, 16)
            sp.dma_start(iota[:], d["iota"]).then_inc(w_in, 16)
            sp.wait_ge(combT_done, NC)
            sp.dma_start(comb_scratch, combT[0:NE + 1, :]).then_inc(stored, 16)
            sp.wait_ge(stored, 16)

        @block.scalar
        def _(act):
            act.wait_ge(w_in, 48)
            nc.scalar.copy(wo_hi[:], wo[:]).then_inc(w_hi_done, 1)
            nc.scalar.copy(wr_hi[:], wr[:]).then_inc(w_hi_done, 1)
            norm.on_scalar(act)
            for k in range(KT):
                for c in range(NC):
                    act.wait_ge(x_transposed, k * NC + c + 1)
                    nc.scalar.copy(acc[:, k, c * CH:(c + 1) * CH], bank[:, k * NC + c, :]).then_inc(acc_done, 1)
            for k in range(KT):
                for c in range(NC):
                    act.wait_ge(n_transposed, k * NC + c + 1)
                    nc.scalar.copy(xT_hi[:, k, c * CH:(c + 1) * CH], bank[:, 4 + k * NC + c, :]
                                   ).then_inc(xT_hi_done, 1)
            act.wait_ge(routed, 1)
            nc.scalar.copy(logits[:], bank[:, 0, 0:NT * NR].rearrange("p (j r) -> p j r", j=NT)
                           ).then_inc(logits_out, 1)
            act.wait_ge(step, SHIFT_STEP)
            nc.scalar.activation(expd[:], shifted[:], ACT.Exp).then_inc(exps, 1)
            act.wait_ge(logits_out, 1)
            nc.scalar.activation(row["ez"][:], logits[:, :, NE:NE + 1], ACT.Exp, scale=-1.0).then_inc(exps, 1)
            for c in range(NC):
                act.wait_ge(comb_transposed, c + 1)
                nc.scalar.copy(combT[:, c * CH:(c + 1) * CH], bank[0:64, 1 + c, :]).then_inc(combT_done, 1)

        @block.vector
        def _(dve):
            dve.wait_ge(w_hi_done, 1)
            nc.vector.tensor_tensor(wo_lo[:], wo[:], wo_hi[:].bitcast(F32), ALU.subtract).then_inc(w_lo_done, 1)
            dve.wait_ge(w_hi_done, 2)
            nc.vector.tensor_tensor(wr_lo[:], wr[:], wr_hi[:].bitcast(F32), ALU.subtract).then_inc(w_lo_done, 1)
            for j in range(NT):
                dve.wait_ge(projected, j + 1)
                nc.vector.tensor_tensor(x[:, j, :], bank[:, j, 0:D], x[:, j, :], ALU.add).then_inc(joined, 1)
            dve.wait_ge(joined, NT)
            norm.on_vector(dve, x, xn)
            for k in range(KT):
                for c in range(NC):
                    dve.wait_ge(xT_hi_done, k * NC + c + 1)
                    cols = slice(c * CH, (c + 1) * CH)
                    nc.vector.tensor_tensor(xT_lo[:, k, cols], bank[:, 4 + k * NC + c, :],
                                            xT_hi[:, k, cols].bitcast(F32), ALU.subtract).then_inc(xT_lo_done, 1)

            count = [0]

            def chained(ins):
                ins.then_inc(step, 1)
                count[0] += 1
                dve.wait_ge(step, count[0])

            dve.wait_ge(logits_out, 1)
            experts = logits[:, :, 0:NE]
            chained(nc.vector.tensor_reduce(row["mx"][:], experts, AX_X, ALU.max))
            chained(nc.vector.tensor_tensor(shifted[:], experts, row["mx"][:].to_broadcast([P, NT, NE]), ALU.subtract))
            assert count[0] == SHIFT_STEP
            dve.wait_ge(exps, 1)
            chained(nc.vector.tensor_reduce(row["sum"][:], expd[:], AX_X, ALU.add))
            chained(nc.vector.reciprocal(row["inv"][:], row["sum"][:]))
            chained(nc.vector.tensor_tensor(soft[:], expd[:], row["inv"][:].to_broadcast([P, NT, NE]), ALU.mult))
            for j in range(NT):
                chained(nc.vector.max(top[:, j, :], soft[:, j, :]))
            for j in range(NT):
                chained(nc.vector.max_index(top_id[:, j, :], top[:, j, :], soft[:, j, :]))
            chained(nc.vector.tensor_copy(top_idf[:], top_id[:]))
            chained(nc.vector.tensor_reduce(row["sum4"][:], top[:, :, 0:TOPK], AX_X, ALU.add))
            chained(nc.vector.tensor_scalar(row["sum4e"][:], row["sum4"][:], 1e-20, None, ALU.add))
            chained(nc.vector.reciprocal(row["inv4"][:], row["sum4e"][:]))
            chained(nc.vector.scalar_tensor_tensor(top_w[:, :, 0:TOPK], top[:, :, 0:TOPK], 0.5,
                                                   row["inv4"][:].to_broadcast([P, NT, TOPK]), ALU.mult, ALU.mult))
            chained(nc.vector.memset(comb[:], 0.0))
            for k in range(TOPK):
                chained(nc.vector.tensor_tensor(
                    hit[:], iota[:].rearrange("p (o e) -> p o e", o=1).to_broadcast([P, NT, NE]),
                    top_idf[:, :, k:k + 1].to_broadcast([P, NT, NE]), ALU.is_equal))
                chained(nc.vector.tensor_tensor(hitw[:], hit[:], top_w[:, :, k:k + 1].to_broadcast([P, NT, NE]), ALU.mult))
                chained(nc.vector.tensor_tensor(comb[:, :, 0:NE], comb[:, :, 0:NE], hitw[:], ALU.add))
            dve.wait_ge(exps, 2)
            chained(nc.vector.tensor_scalar(row["ez1"][:], row["ez"][:], 1.0, None, ALU.add))
            chained(nc.vector.reciprocal(row["gate"][:], row["ez1"][:]))
            chained(nc.vector.tensor_scalar(comb[:, :, NE:NE + 1], row["gate"][:], 0.5, None, ALU.mult))
            assert count[0] == ROUTE_STEPS

        @block.tensor
        def _(pe):
            pe.wait_ge(w_lo_done, 1)
            for j in range(NT):
                rows = slice(j * P, (j + 1) * P)
                for g in range(NG):
                    for n, (a, b) in enumerate(three((heads_hi, wo_hi), (heads_lo, wo_hi), (heads_hi, wo_lo))):
                        last = nc.tensor.matmul(bank[:, j, 0:D], a[:, g, rows], b[:, g, :],
                                                start=(g == 0 and n == 0), stop=(g == NG - 1 and n == 2))
                last.then_inc(projected, 1)

            def transpose_all(src, first, done, ready):
                for k in range(KT):
                    for j in range(NT):
                        ready(k, j)
                        last = nc.tensor.transpose(bank[:, first + k * NC + j // TPC, (j % TPC) * P:(j % TPC + 1) * P],
                                                   src[:, j, k * P:(k + 1) * P], ident[:])
                        if j % TPC == TPC - 1:
                            last.then_inc(done, 1)

            transpose_all(x, 0, x_transposed, lambda k, j: pe.wait_ge(joined, NT))
            transpose_all(xn, 4, n_transposed,
                          lambda k, j: pe.wait_ge(norm.step, norm.DONE + (j + 1 if k == 0 else NT)))
            pe.wait_ge(xT_lo_done, KT * NC)
            pe.wait_ge(w_lo_done, 2)
            pe.wait_ge(acc_done, 1)
            for j in range(NT):
                rows = slice(j * P, (j + 1) * P)
                for k in range(KT):
                    for n, (a, b) in enumerate(three((xT_hi, wr_hi), (xT_lo, wr_hi), (xT_hi, wr_lo))):
                        last = nc.tensor.matmul(bank[:, 0, j * NR:(j + 1) * NR], a[:, k, rows], b[:, k, :],
                                                start=(k == 0 and n == 0), stop=(k == KT - 1 and n == 2))
            last.then_inc(routed, 1)
            pe.wait_ge(step, ROUTE_STEPS)
            pe.wait_ge(acc_done, 3)
            for j in range(NT):
                last = nc.tensor.transpose(bank[0:64, 1 + j // TPC, (j % TPC) * P:(j % TPC + 1) * P],
                                           comb[:, j, :], ident[:])
                if j % TPC == TPC - 1:
                    last.then_inc(comb_transposed, 1)


def layer1(nc, d, ctx, sb, bank, ident, ident_bf, mask_bf, xT_hi, xT_lo, acc, comb_scratch):
    sem = Semaphores(nc, ctx, "d_")

    def buf(name, shape, dt=F32):
        return sb("d_" + name, shape, dt, on=ctx)

    QKV, GU = KT * 3 * P, KT * 2 * P
    cos, sin = buf("cos", [P, T]), buf("sin", [P, T])
    gl, ge, g1, gs = buf("gl", [P, H1]), buf("ge", [P, H1]), buf("g1", [P, H1]), buf("gs", [P, H1])
    gs_now = buf("gs_now", [P, 1])
    qkv_raw, qkv_hi, qkv_lo = buf("qkv_raw", [P, QKV]), buf("qkv_hi", [P, QKV], F32R), buf("qkv_lo", [P, QKV], F32R)
    gu_raw = buf("gu_raw", [P, GU])
    gu_hi = [buf(f"gu_hi{t}", [P, GU], F32R) for t in range(ET)]
    gu_lo = [buf(f"gu_lo{t}", [P, GU], F32R) for t in range(ET)]
    ow_raw = buf("ow_raw", [P, 3, D])
    ow_hi, ow_lo = buf("ow_hi", [P, 3, D], F32R), buf("ow_lo", [P, 3, D], F32R)
    cb = buf("cb", [P, T])
    qk_hi = {w: buf(f"{w}_hi", [P, T], F32R) for w in "qk"}
    qk_lo = {w: buf(f"{w}_lo", [P, T], F32R) for w in "qk"}
    swap = buf("swap", [P, CH])
    rot = [buf(f"rot{n}", [P, CH]) for n in range(2)]
    v_hi, v_lo = buf("v_hi", [P, NT, DV], F32R), buf("v_lo", [P, NT, DV], F32R)
    NP_ = 4
    probs = [buf(f"probs{n}", [P, T]) for n in range(NP_)]
    neg_max, row_sum, row_inv = (buf(n, [P, HPI * NT]) for n in ("neg_max", "row_sum", "row_inv"))
    pT_hi = [buf(f"pT_hi{c}", [P, (c + 1) * TPC, CH], F32R) for c in range(NC)]
    pT_lo = [buf(f"pT_lo{c}", [P, (c + 1) * TPC, CH], F32R) for c in range(NC)]
    head_hi, head_lo = buf("head_hi", [P, T], F32R), buf("head_lo", [P, T], F32R)
    tanh = [buf(f"tanh{n}", [P, CH]) for n in range(2)]
    g_act, gu_act = buf("g_act", [P, CH]), buf("gu_act", [P, CH])
    hid = [buf(f"hid{n}", [P, CH]) for n in range(2)]
    hid_hi, hid_lo = buf("hid_hi", [P, 2, T], F32R), buf("hid_lo", [P, 2, T], F32R)

    const_in, gate_step = sem("const_in"), sem("gate_step")
    qkv_in, gu_in, ow_in, cb_in = sem("qkv_in"), sem("gu_in"), sem("ow_in"), sem("cb_in")
    qkv_hi_done, qkv_lo_done, gu_hi_done, gu_lo_done, ow_hi_done, ow_lo_done = (
        sem(n) for n in ("qkv_hi_done", "qkv_lo_done", "gu_hi_done", "gu_lo_done", "ow_hi_done", "ow_lo_done"))
    unit_done = sem("unit_done")
    unit_free = sem("unit_free")
    rope_step, rotated, qk_hi_done, qk_lo_done = (
        sem(n) for n in ("rope_step", "rotated", "qk_hi_done", "qk_lo_done"))
    v_hi_done, inverted_seen = sem("v_hi_done"), sem("inverted_seen")
    scored, maxed, exped, inverted, normed = (sem(n) for n in ("scored", "maxed", "exped", "inverted", "normed"))
    transposed, pT_hi_done, pT_lo_done = sem("transposed"), sem("pT_hi_done"), sem("pT_lo_done")
    head_hi_done = sem("head_hi_done")
    tanh_done, hid_done, hid_hi_done, hid_lo_done = (
        sem(n) for n in ("tanh_done", "hid_done", "hid_hi_done", "hid_lo_done"))
    out_done = sem("out_done")

    S_BANK, T_BANK, U_BANK = 0, 4, 6

    NEXT = ("qk", "v")
    PE_ORDER = (
        "S2 T0 S3 pair0 T1 S4 pair1 T2 S5 qk0 T3 S6 pair2 S7 T4 T5 qk1 pv0 T6 T7 qk2 pv1 v0 qk3 S8 "
        "v1 S9 out0 out1 out2 out3")
    ACT_ORDER = (
        "qkv T0 S2 pair0 S3 ow T1 hid0 pair1 gu_mid S4 T2 S5 T3 hid1 pair2 qk0 T4 T5 S6 S7 pv0 T6 "
        "T7 hid2 qk1 gu_end pv1 qk2 v0 v1 S8 S9 qk3")
    DVE_ORDER = (
        "S2 T0 S3 pair0 inv2 S4 T1 inv3 pair1 S5 inv4 T2 qk0 inv5 T3 pair2 S6 S7 T4 inv6 T5 inv7 "
        "qk1 pv0 T6 T7 qk2 pv1 v0 S8 qk3 v1 out0 S9 out1 out2 inv8 inv9 out3")
    POOL_ORDER = (
        "S2 qkv S3 hid0 gu_mid S4 S5 hid1 S6 S7 qk0 ow qk1 gu_end qk2 hid2 S8 S9 qk3")
    QK_OF = [("q", 1), ("k", 1), ("k", 0), ("q", 0)]
    PV_CHUNK = [1, 0]
    TILE = [NT - 1 - n for n in range(NT)]
    UNITS_T = [(n, j, min(4, TILE[n] + 1 - j)) for n in range(NT) for j in range(0, TILE[n] + 1, 4)]
    UNITS_OF = [[u for u, t in enumerate(UNITS_T) if t[0] == n] for n in range(NT)]

    def steps(order, last_head):
        for step in order.split():
            name, n = step.rstrip("0123456789"), int("0" + step.lstrip("SabcdefghijklmnopqrstuvwxyzT_"))
            if last_head and (name in NEXT or name == "qkv" or (name in ("S", "inv") and n >= NT)):
                continue
            yield name, n

    QK_UNITS, V_UNITS, PV_UNITS, OUT_UNITS, NPAIR = 2 * NC, NT // TPC, NC, KT * NC, 3

    def unit_places(last_head):
        places, at = {}, 0
        for name, n in steps(PE_ORDER, last_head):
            if name not in ("S", "T"):
                places[name, n] = at
                at += 2 if name == "pair" else 1
        return places, at

    PLACES, HEAD_UNITS = unit_places(False)
    LAST_PLACES, LAST_UNITS = unit_places(True)
    PAIRS = [[(0, 0), (0, 1), (1, 0)], [(1, 1), (2, 0), (2, 1)]]
    GU_MID = [(0, PLACES["pair", 1] + 2), (1, PLACES["pair", 0] + 2)]
    GU_END = [None, (2, PLACES["pair", 2] + 2)]
    GU_BEFORE = [0, 1]
    HID_BUF = [0, 1, 0]
    OUT_TILES = [[0], [1, 2]]
    OW = [1 + len(t) for t in OUT_TILES]

    SHARED_PAIRS = ST * NC
    HALF_UNITS = 2 * 2 * NC + OUT_UNITS
    QK0_UNIT = HALF_UNITS + 2 * 2 * NC
    SHARED_OUT = [2 * 2 * NC, QK0_UNIT + QK_UNITS]
    V0_UNIT = SHARED_OUT[1] + OUT_UNITS
    LOOP0 = V0_UNIT + V_UNITS
    assert LOOP0 % 2 == 0 and HEAD_UNITS % 2 == 0 and all(u % 2 == 0 for u in SHARED_OUT + [QK0_UNIT, V0_UNIT])
    GU0 = ST + ET
    SHARED_BUF = [2, 0, 1, 2]

    class Head:

        def __init__(self, it, hh, last):
            self.hh, self.last_head = hh, last and hh == HPI - 1
            self.last_round = last
            self.h = it * HPI + hh
            self.unit = it * (HPI * HEAD_UNITS) + (LOOP0 + hh * HEAD_UNITS)
            self.slot = it * (HPI * NT) + hh * NT
            self.tu = it * (HPI * NTU) + hh * NTU
            self.pair = it * (HPI * NPAIR) + (SHARED_PAIRS + hh * NPAIR)
            self.qk = it * (HPI * QK_UNITS) + (hh + 1) * QK_UNITS
            self.v = it * (HPI * V_UNITS) + (hh + 1) * V_UNITS
            self.gu = it * ET + (GU0 + GU_BEFORE[hh])
            self.places = LAST_PLACES if self.last_head else PLACES
            self.units = LAST_UNITS if self.last_head else HEAD_UNITS

        def first_unit(self, name, n):
            return self.unit + self.places[name, n]

        def col(self, s):
            n = (self.hh * NT + s) % (HPI * NT)
            return slice(n, n + 1)

    class Before:
        hh, slot = HPI - 1, -NT
        col = Head.col

    before = Before()

    def unit_bank(place):
        return bank[:, U_BANK + place % 2, :]

    def score_bank(s, w):
        return bank[:, S_BANK + 2 * (s % 2):S_BANK + 2 * (s % 2) + 2, :].rearrange("p b t -> p (b t)")[:, 0:w]

    def width(s):
        return (TILE[s % NT] + 1) * P

    def rounds(engine, body):
        with engine.Fori(0, NEG - 1) as it:
            for hh in range(HPI):
                body(Head(it, hh, False), it)
        for hh in range(HPI):
            body(Head(NEG - 1, hh, True), NEG - 1)

    with nc.Block() as block:
        @block.sync
        def _(sp):
            sp.dma_start(gu_raw[:], d["gu_shared"][0]).then_inc(gu_in, 16)
            sp.dma_start(ow_raw[:, 0:2, :], d["down_shared"][0]).then_inc(ow_in, 16)
            sp.dma_start(cb[:], comb_scratch[NE:NE + 1, :].to_broadcast([P, T])).then_inc(cb_in, 16)
            sp.dma_start(gl[:], d["gate_logit"]).then_inc(const_in, 16)
            sp.dma_start(cos[:], d["cos1"]).then_inc(const_in, 16)
            sp.dma_start(sin[:], d["sin1"]).then_inc(const_in, 16)
            sp.dma_start(qkv_raw[:], d["w_qkv1"][0]).then_inc(qkv_in, 16)
            for n in range(1, GU0):
                sp.wait_ge(gu_hi_done, n)
                sp.wait_ge(gu_lo_done, n)
                sp.dma_start(gu_raw[:], d["gu_shared"][n] if n < ST else d["gu1"][n - ST]).then_inc(gu_in, 16)
                if n == ST - 1:
                    sp.wait_ge(ow_hi_done, 1)
                    sp.wait_ge(ow_lo_done, 1)
                    sp.dma_start(ow_raw[:, 0:2, :], d["down_shared"][1]).then_inc(ow_in, 16)

            d_comb = comb_scratch[0:NE, :].rearrange("(g e o) t -> g e o t", e=EG, o=1).to_broadcast(
                [NEG, EG, P // EG, T])

            def body(h, it):
                if h.hh == 0:
                    sp.wait_ge(hid_done, h.pair)
                    sp.dma_start(cb[:], d_comb[bass.ds(it, 1)].rearrange("o e r t -> (o e) r t")).then_inc(cb_in, 16)
                if not h.last_head:
                    sp.wait_ge(qkv_hi_done, h.h + 1)
                    sp.wait_ge(qkv_lo_done, h.h + 1)
                    sp.dma_start(qkv_raw[:], d["w_qkv1"][bass.ds(h.h + 1, 1)].rearrange("o p n -> (o p) n")
                                 ).then_inc(qkv_in, 16)
                sp.wait_ge(ow_hi_done, h.h + ST // 2)
                sp.wait_ge(ow_lo_done, h.h + ST // 2)
                src = (d["ow_a"] if h.hh == 0 else d["ow_b"])[bass.ds(it, 1)].rearrange("o p t n -> (o p) t n")
                sp.dma_start(ow_raw[:, 0:OW[h.hh], :], src).then_inc(ow_in, 16)
                if not h.last_round:
                    for n, split in enumerate((GU_MID[h.hh], GU_END[h.hh])):
                        if split is not None:
                            sp.wait_ge(gu_hi_done, h.gu + n)
                            sp.wait_ge(gu_lo_done, h.gu + n)
                            sp.dma_start(gu_raw[:], d["gu1"][bass.ds((it + 1) * ET + split[0], 1)]
                                         .rearrange("o p n -> (o p) n")).then_inc(gu_in, 16)

            rounds(sp, body)
            sp.wait_ge(unit_free, Head(NEG - 1, HPI - 1, True).unit + LAST_UNITS)
            for k in range(KT):
                sp.dma_start(d["out"][k], acc[:, k, :]).then_inc(out_done, 16)
            sp.wait_ge(out_done, 16 * KT)

        @block.scalar
        def _(act):
            def part_hi(dst, src, raw_in, raw_n, used_units, done):
                act.wait_ge(raw_in, raw_n)
                if used_units is not None:
                    act.wait_ge(unit_done, used_units)
                nc.scalar.copy(dst, src).then_inc(done, 1)

            def tanh_gate(pair, par, unit, place):
                act.wait_ge(unit_done, unit + 1)
                act.wait_ge(hid_done, pair - 1)
                nc.scalar.activation(tanh[par][:], unit_bank(place), ACT.Tanh, scale=0.5).then_inc(tanh_done, 1)

            def hidden_hi(pair, par, buf_n, c, out_free):
                act.wait_ge(hid_done, pair + 1)
                act.wait_ge(unit_done, out_free)
                nc.scalar.copy(hid_hi[:, buf_n, c * CH:(c + 1) * CH], hid[par][:]).then_inc(hid_hi_done, 1)

            def qk_part_hi(count, n):
                w, c = QK_OF[n]
                act.wait_ge(rotated, count + n + 1)
                nc.scalar.copy(qk_hi[w][:, c * CH:(c + 1) * CH], rot[n % 2][:]).then_inc(qk_hi_done, 1)

            def v_part_hi(unit, n, place):
                act.wait_ge(unit_done, unit + 1)
                nc.scalar.copy(v_hi[:, n * TPC:(n + 1) * TPC, :],
                               unit_bank(place).rearrange("p (j e) -> p j e", j=TPC)).then_inc(v_hi_done, 1)

            def exp(h, s):
                act.wait_ge(maxed, h.slot + s + 1)
                nc.scalar.activation(probs[s % NP_][:, 0:width(s)], score_bank(s, width(s)), ACT.Exp,
                                     bias=neg_max[:, h.col(s)], accum_out=row_sum[:, h.col(s)]).then_inc(exped, 1)

            def gu_part_hi(n):
                b = SHARED_BUF[n] if n < ST else n - ST
                used = {ST - 1: 2 * NC, ST: 2 * 2 * NC, ST + 1: HALF_UNITS + 2 * NC, ST + 2: QK0_UNIT}.get(n)
                part_hi(gu_hi[b][:], gu_raw[:], gu_in, 16 * (n + 1), used, gu_hi_done)

            gu_part_hi(0)
            part_hi(ow_hi[:, 0:2, :], ow_raw[:, 0:2, :], ow_in, 16, None, ow_hi_done)
            act.wait_ge(const_in, 48)
            nc.scalar.activation(ge[:], gl[:], ACT.Exp, scale=-1.0).then_inc(gate_step, 1)
            for t in range(ST):
                half = t // 2
                u0 = half * HALF_UNITS + (t % 2) * 2 * NC
                for c in range(NC):
                    p = t * NC + c
                    act.wait_ge(unit_done, u0 + 2 * c + 1)
                    if p >= 2:
                        act.wait_ge(hid_done, p - 1)
                    nc.scalar.activation(tanh[p % 2][:], unit_bank(0), ACT.Tanh, scale=0.5).then_inc(tanh_done, 1)
                    if c == 0:
                        gu_part_hi(t + 1)
                    if t == 1 and c == 0:
                        part_hi(qkv_hi[:], qkv_raw[:], qkv_in, 16, None, qkv_hi_done)
                    hidden_hi(p, p % 2, t % 2, c, half * HALF_UNITS)
                if t == 2:
                    part_hi(ow_hi[:, 0:2, :], ow_raw[:, 0:2, :], ow_in, 32, HALF_UNITS, ow_hi_done)
            for n in range(QK_UNITS):
                qk_part_hi(0, n)
                if n < ET - 1:
                    gu_part_hi(ST + 1 + n)
            exp(before, NT)
            for n in range(V_UNITS):
                v_part_hi(V0_UNIT + n, n, n)
            exp(before, NT + 1)

            def body(h, it):
                for name, n in steps(ACT_ORDER, h.last_head):
                    if name == "S":
                        if n >= NP_:
                            act.wait_ge(transposed, h.tu + UNITS_OF[n - NP_][-1] + 1)
                        exp(h, n)
                    elif name == "T":
                        for tu in UNITS_OF[n]:
                            _, j, blocks = UNITS_T[tu]
                            c, col = TILE[n] // TPC, (TILE[n] % TPC) * P
                            act.wait_ge(transposed, h.tu + tu + 1)
                            nc.scalar.copy(pT_hi[c][:, j:j + blocks, col:col + P],
                                           bank[:, T_BANK + tu % 2, 0:blocks * P].rearrange("p (b q) -> p b q", b=blocks)
                                           ).then_inc(pT_hi_done, 1)
                    elif name == "pair":
                        tanh_gate(h.pair + n, (h.hh + n) % 2, h.first_unit("pair", n), h.places["pair", n])
                    elif name == "hid":
                        tile, c = PAIRS[h.hh][n]
                        hidden_hi(h.pair + n, (h.hh + n) % 2, HID_BUF[tile], c, h.unit)
                    elif name == "qk":
                        qk_part_hi(h.qk, n)
                    elif name == "v":
                        v_part_hi(h.first_unit("v", n), n, h.places["v", n])
                    elif name == "pv":
                        act.wait_ge(unit_done, h.first_unit("pv", n) + 1)
                        c = PV_CHUNK[n]
                        nc.scalar.copy(head_hi[:, c * CH:(c + 1) * CH], unit_bank(h.places["pv", n])
                                       ).then_inc(head_hi_done, 1)
                    elif name == "ow":
                        part_hi(ow_hi[:, 0:OW[h.hh], :], ow_raw[:, 0:OW[h.hh], :], ow_in,
                                (h.h + ST // 2) * 16 + 16, h.unit, ow_hi_done)
                    elif name == "qkv":
                        part_hi(qkv_hi[:], qkv_raw[:], qkv_in, h.h * 16 + 32, h.unit, qkv_hi_done)
                    elif not h.last_round:
                        at = ("gu_mid", "gu_end").index(name)
                        split = (GU_MID, GU_END)[at][h.hh]
                        if split is not None:
                            part_hi(gu_hi[split[0]][:], gu_raw[:], gu_in, (h.gu + at) * 16 + 16, h.unit + split[1],
                                    gu_hi_done)

            rounds(act, body)

        @block.vector
        def _(dve):
            def pair_steps(pair, par, c, unit, place, hid_free):
                dve.wait_ge(tanh_done, pair + 1)
                dve.wait_ge(hid_done, pair)
                nc.vector.scalar_tensor_tensor(g_act[:], tanh[par][:], 1.0, unit_bank(place), ALU.add, ALU.mult
                                               ).then_inc(unit_free, 1)
                dve.wait_ge(unit_done, unit + 2)
                dve.wait_ge(unit_free, unit + 1)
                nc.vector.tensor_tensor(gu_act[:], g_act[:], unit_bank(place + 1), ALU.mult).then_inc(unit_free, 1)
                dve.wait_ge(unit_free, unit + 2)
                dve.wait_ge(hid_lo_done, hid_free)
                nc.vector.tensor_tensor(hid[par][:], gu_act[:], cb[:, c * CH:(c + 1) * CH], ALU.mult
                                        ).then_inc(hid_done, 1)

            def out_add(unit, n, place):
                k, c = n // NC, PV_CHUNK[n % NC]
                dve.wait_ge(unit_done, unit + 1)
                dve.wait_ge(unit_free, unit)
                nc.vector.tensor_tensor(acc[:, k, c * CH:(c + 1) * CH], acc[:, k, c * CH:(c + 1) * CH],
                                        unit_bank(place), ALU.add).then_inc(unit_free, 1)

            def rope(unit, count, n, place, first=False):
                (w, c), src = QK_OF[n], unit_bank(place)
                cols = slice(c * CH, (c + 1) * CH)

                def product(dst, rows, table):
                    if w == "q":
                        return nc.vector.scalar_tensor_tensor(dst, src[rows, :], gs_now[rows, 0:1], table[rows, cols],
                                                              ALU.mult, ALU.mult)
                    return nc.vector.tensor_tensor(dst, src[rows, :], table[rows, cols], ALU.mult)

                low, high = slice(DS, DS + 32), slice(DS + 32, P)
                dve.wait_ge(unit_done, unit + 1)
                if n >= 1 or not first:
                    dve.wait_ge(rotated, count + n)
                product(swap[low, :], high, sin).then_inc(rope_step, 1)
                product(swap[high, :], low, sin).then_inc(rope_step, 1)
                if n >= 2 or not first:
                    dve.wait_ge(qk_lo_done, count + n - 1)
                product(rot[n % 2][:], slice(0, P), cos).then_inc(unit_free, 1)
                dve.wait_ge(rope_step, (count + n) * 2 + 2)
                dve.wait_ge(unit_free, unit + 1)
                nc.vector.tensor_tensor(rot[n % 2][DS:P, :], rot[n % 2][DS:P, :], swap[DS:P, :], ALU.add
                                        ).then_inc(rotated, 1)

            def v_part_lo(count, n, place):
                dve.wait_ge(v_hi_done, count + n + 1)
                nc.vector.tensor_tensor(v_lo[:, n * TPC:(n + 1) * TPC, :],
                                        unit_bank(place).rearrange("p (j e) -> p j e", j=TPC),
                                        v_hi[:, n * TPC:(n + 1) * TPC, :].bitcast(F32), ALU.subtract
                                        ).then_inc(unit_free, 1)

            def maximum(h, s):
                dve.wait_ge(scored, h.slot + s + 1)
                nc.vector.tensor_reduce(neg_max[:, h.col(s)], score_bank(s, width(s)), AX_X, ALU.max, negate=True
                                        ).then_inc(maxed, 1)

            def inverse(h, s):
                dve.wait_ge(exped, h.slot + s + 1)
                nc.vector.reciprocal(row_inv[:, h.col(s)], row_sum[:, h.col(s)]).then_inc(inverted, 1)

            scale = float(DS) ** -0.5
            dve.wait_ge(gate_step, 1)
            nc.vector.tensor_scalar(g1[:], ge[:], 1.0, None, ALU.add).then_inc(gate_step, 1)
            dve.wait_ge(gate_step, 2)
            nc.vector.reciprocal(ge[:], g1[:]).then_inc(gate_step, 1)
            dve.wait_ge(gate_step, 3)
            nc.vector.tensor_scalar(gs[0:DS, :], ge[0:DS, :], scale, None, ALU.mult)
            nc.vector.tensor_scalar(gs[DS:P, :], ge[DS:P, :], -scale, scale, ALU.mult, ALU.add).then_inc(gate_step, 1)
            dve.wait_ge(gate_step, 4)
            nc.vector.tensor_copy(gs_now[:], gs[:, 0:1]).then_inc(gate_step, 1)

            dve.wait_ge(cb_in, 16)
            for a in range(2):
                for q in range(2 * NC):
                    p = a * 2 * NC + q
                    pair_steps(p, p % 2, q % NC, a * HALF_UNITS + 2 * q, 0, max(0, p - 1))
                if a:
                    dve.wait_ge(gate_step, 5)
                    for n in range(QK_UNITS):
                        rope(QK0_UNIT + n, 0, n, n, first=True)
                for n in range(OUT_UNITS):
                    out_add(SHARED_OUT[a] + n, n, n)
            maximum(before, NT)
            for n in range(V_UNITS):
                v_part_lo(0, n, n)
            inverse(before, NT)
            maximum(before, NT + 1)
            inverse(before, NT + 1)

            def body(h, it):
                if h.hh == 0:
                    dve.wait_ge(cb_in, it * 16 + 32)
                for name, n in steps(DVE_ORDER, h.last_head):
                    if name == "S":
                        maximum(h, n)
                    elif name == "inv":
                        inverse(h, n)
                    elif name == "T":
                        for tu in UNITS_OF[n]:
                            _, j, blocks = UNITS_T[tu]
                            c, col = TILE[n] // TPC, (TILE[n] % TPC) * P
                            dve.wait_ge(pT_hi_done, h.tu + tu + 1)
                            nc.vector.tensor_tensor(pT_lo[c][:, j:j + blocks, col:col + P],
                                                    bank[:, T_BANK + tu % 2, 0:blocks * P].rearrange(
                                                        "p (b q) -> p b q", b=blocks),
                                                    pT_hi[c][:, j:j + blocks, col:col + P].bitcast(F32), ALU.subtract
                                                    ).then_inc(pT_lo_done, 1)
                    elif name == "pair":
                        pair_steps(h.pair + n, (h.hh + n) % 2, PAIRS[h.hh][n][1], h.first_unit("pair", n),
                                   h.places["pair", n], h.pair + n - 1)
                    elif name == "qk":
                        if n == 0:
                            dve.wait_ge(rotated, h.qk)
                            dve.wait_ge(gate_step, h.h + 5)
                            nc.vector.tensor_copy(gs_now[:], gs[:, bass.ds(h.h + 1, 1)]).then_inc(gate_step, 1)
                            dve.wait_ge(gate_step, h.h + 6)
                        rope(h.first_unit("qk", n), h.qk, n, h.places["qk", n])
                    elif name == "v":
                        v_part_lo(h.v, n, h.places["v", n])
                    elif name == "pv":
                        dve.wait_ge(head_hi_done, h.h * PV_UNITS + n + 1)
                        cols = slice(PV_CHUNK[n] * CH, (PV_CHUNK[n] + 1) * CH)
                        nc.vector.tensor_tensor(head_lo[:, cols], unit_bank(h.places["pv", n]),
                                                head_hi[:, cols].bitcast(F32), ALU.subtract).then_inc(unit_free, 1)
                    elif name == "out":
                        out_add(h.first_unit("out", n), n, h.places["out", n])

            rounds(dve, body)

        @block.gpsimd
        def _(pool):
            def part_lo(dst, src, hi, hi_done, n, done):
                pool.wait_ge(hi_done, n)
                nc.gpsimd.tensor_tensor(dst, src, hi.bitcast(F32), ALU.subtract).then_inc(done, 1)

            def hidden_lo(pair, par, buf_n, c):
                pool.wait_ge(hid_hi_done, pair + 1)
                cols = slice(c * CH, (c + 1) * CH)
                nc.gpsimd.tensor_tensor(hid_lo[:, buf_n, cols], hid[par][:], hid_hi[:, buf_n, cols].bitcast(F32),
                                        ALU.subtract).then_inc(hid_lo_done, 1)

            def qk_part_lo(count, n):
                w, c = QK_OF[n]
                cols = slice(c * CH, (c + 1) * CH)
                pool.wait_ge(qk_hi_done, count + n + 1)
                nc.gpsimd.tensor_tensor(qk_lo[w][:, cols], rot[n % 2][:], qk_hi[w][:, cols].bitcast(F32),
                                        ALU.subtract).then_inc(qk_lo_done, 1)

            def normalise(h, s):
                pool.wait_ge(inverted, h.slot + s + 1)
                pool.sem_inc(inverted_seen)
                nc.gpsimd.tensor_scalar(probs[s % NP_][:, 0:width(s)], probs[s % NP_][:, 0:width(s)],
                                        row_inv[:, h.col(s)], 1.0, ALU.mult, ALU.mult).then_inc(normed, 1)

            def gu_part_lo(n):
                b = SHARED_BUF[n] if n < ST else n - ST
                part_lo(gu_lo[b][:], gu_raw[:], gu_hi[b][:], gu_hi_done, n + 1, gu_lo_done)

            gu_part_lo(0)
            part_lo(ow_lo[:, 0:2, :], ow_raw[:, 0:2, :], ow_hi[:, 0:2, :], ow_hi_done, 1, ow_lo_done)
            for t in range(ST):
                for c in range(NC):
                    if c == 0:
                        gu_part_lo(t + 1)
                    if t == 1 and c == 0:
                        part_lo(qkv_lo[:], qkv_raw[:], qkv_hi[:], qkv_hi_done, 1, qkv_lo_done)
                    hidden_lo(t * NC + c, (t * NC + c) % 2, t % 2, c)
                if t == 2:
                    part_lo(ow_lo[:, 0:2, :], ow_raw[:, 0:2, :], ow_hi[:, 0:2, :], ow_hi_done, 2, ow_lo_done)
            for n in range(QK_UNITS):
                qk_part_lo(0, n)
                if n < ET - 1:
                    gu_part_lo(ST + 1 + n)
            normalise(before, NT)
            normalise(before, NT + 1)

            def body(h, it):
                for name, n in steps(POOL_ORDER, h.last_head):
                    if name == "S":
                        normalise(h, n)
                    elif name == "hid":
                        tile, c = PAIRS[h.hh][n]
                        hidden_lo(h.pair + n, (h.hh + n) % 2, HID_BUF[tile], c)
                    elif name == "qk":
                        qk_part_lo(h.qk, n)
                    elif name == "ow":
                        blocks = slice(0, OW[h.hh])
                        part_lo(ow_lo[:, blocks, :], ow_raw[:, blocks, :], ow_hi[:, blocks, :], ow_hi_done,
                                h.h + ST // 2 + 1, ow_lo_done)
                    elif name == "qkv":
                        part_lo(qkv_lo[:], qkv_raw[:], qkv_hi[:], qkv_hi_done, h.h + 2, qkv_lo_done)
                    elif not h.last_round:
                        at = ("gu_mid", "gu_end").index(name)
                        split = (GU_MID, GU_END)[at][h.hh]
                        if split is not None:
                            part_lo(gu_lo[split[0]][:], gu_raw[:], gu_hi[split[0]][:], gu_hi_done, h.gu + at + 1,
                                    gu_lo_done)

            rounds(pool, body)

        @block.tensor
        def _(pe):
            def w_slice(w, k, part):
                return w[:, (k * 3 + part) * P:(k * 3 + part + 1) * P]

            def project_T(place, parts, c):
                cols = slice(c * CH, (c + 1) * CH)
                for k in range(KT):
                    for n, (a, b) in enumerate(three((0, xT_hi), (1, xT_hi), (0, xT_lo))):
                        last = nc.tensor.matmul(unit_bank(place), parts(a, k), b[:, k, cols],
                                                start=(k == 0 and n == 0), stop=(k == KT - 1 and n == 2))
                last.then_inc(unit_done, 1)

            def pair_units(unit, place, b, c):
                for part in range(2):
                    if unit is not None:
                        pe.wait_ge(unit_free, unit + part - 1)
                    project_T(place + part, lambda a, k: (gu_hi, gu_lo)[a][b][:, (k * 2 + part) * P:
                                                                             (k * 2 + part + 1) * P], c)

            def qk_unit(unit, n, place):
                pe.wait_ge(unit_free, unit - 1)
                w, c = QK_OF[n]
                project_T(place, lambda a, k: w_slice((qkv_hi, qkv_lo)[a], k, "qk".index(w)), c)

            def v_unit(unit, n, place):
                pe.wait_ge(unit_free, unit - 1)
                for jj in range(TPC):
                    j = n * TPC + jj
                    rows = slice(j * P, (j + 1) * P)
                    for k in range(KT):
                        for q, (a, w) in enumerate(three((xT_hi, qkv_hi), (xT_lo, qkv_hi), (xT_hi, qkv_lo))):
                            last = nc.tensor.matmul(unit_bank(place)[:, jj * DV:(jj + 1) * DV], a[:, k, rows],
                                                    w_slice(w, k, 2), start=(k == 0 and q == 0),
                                                    stop=(k == KT - 1 and q == 2))
                last.then_inc(unit_done, 1)

            def out_unit(unit, n, place, products):
                k, c = n // NC, PV_CHUNK[n % NC]
                pe.wait_ge(unit_free, unit - 1)
                rows, cols = slice(k * P, (k + 1) * P), slice(c * CH, (c + 1) * CH)
                todo = [part for blk, hi, lo in products
                        for part in three((ow_hi[:, blk, rows], hi[:, cols]), (ow_lo[:, blk, rows], hi[:, cols]),
                                          (ow_hi[:, blk, rows], lo[:, cols]))]
                for q, (w, m) in enumerate(todo):
                    last = nc.tensor.matmul(unit_bank(place), w, m, start=(q == 0), stop=(q == len(todo) - 1))
                last.then_inc(unit_done, 1)

            def scores(s):
                i = TILE[s % NT]
                for col, w in score_chunks(i):
                    out = bank[:, S_BANK + 2 * (s % 2) + col // CH, 0:w]
                    rows, cols = slice(i * P, (i + 1) * P), slice(col, col + w)
                    diagonal = col + w == (i + 1) * P
                    for n, (a, b) in enumerate(three((qk_hi, qk_hi), (qk_lo, qk_hi), (qk_hi, qk_lo))):
                        last = nc.tensor.matmul(out, a["q"][:, rows], b["k"][:, cols], start=(n == 0),
                                                stop=(n == 2 and not diagonal))
                    if diagonal:
                        last = nc.tensor.matmul(out[:, w - P:w], ident_bf[:], mask_bf[:], start=False, stop=True)
                last.then_inc(scored, 1)

            for a in range(2):
                for t in (2 * a, 2 * a + 1):
                    pe.wait_ge(gu_lo_done, t + 1)
                    for c in range(NC):
                        unit = a * HALF_UNITS + (t % 2) * 2 * NC + 2 * c
                        pair_units(unit if unit else None, 0, SHARED_BUF[t], c)
                if a:
                    pe.wait_ge(qkv_lo_done, 1)
                    for n in range(QK_UNITS):
                        qk_unit(QK0_UNIT + n, n, n)
                pe.wait_ge(hid_lo_done, (a + 1) * 2 * NC)
                pe.wait_ge(ow_lo_done, a + 1)
                for n in range(OUT_UNITS):
                    out_unit(SHARED_OUT[a] + n, n, n, [(b, hid_hi[:, b, :], hid_lo[:, b, :]) for b in range(2)])
            pe.wait_ge(qk_lo_done, 3)
            scores(NT)
            for n in range(V_UNITS):
                v_unit(V0_UNIT + n, n, n)
            scores(NT + 1)

            def body(h, it):
                for name, n in steps(PE_ORDER, h.last_head):
                    unit, place = (h.first_unit(name, n), h.places[name, n]) if (name, n) in h.places else (None, None)
                    if name == "S":
                        if n == TPC:
                            pe.wait_ge(qk_lo_done, h.qk)
                        if n == NT:
                            pe.wait_ge(qk_lo_done, h.qk + 3)
                        pe.wait_ge(exped, h.slot + n - 1)
                        scores(n)
                    elif name == "T":
                        pe.wait_ge(normed, h.slot + n + 1)
                        for tu in UNITS_OF[n]:
                            _, j, blocks = UNITS_T[tu]
                            if tu >= 2:
                                pe.wait_ge(pT_lo_done, h.tu + tu - 1)
                            for b in range(blocks):
                                last = nc.tensor.transpose(bank[:, T_BANK + tu % 2, b * P:(b + 1) * P],
                                                           probs[n % NP_][:, (j + b) * P:(j + b + 1) * P], ident[:])
                            last.then_inc(transposed, 1)
                    elif name == "pair":
                        tile, c = PAIRS[h.hh][n]
                        if c == 0:
                            pe.wait_ge(gu_lo_done, it * ET + (ST + tile + 1))
                        pair_units(unit, place, tile, c)
                    elif name == "qk":
                        if n == 0:
                            pe.wait_ge(qkv_lo_done, h.h + 2)
                        qk_unit(unit, n, place)
                    elif name == "v":
                        v_unit(unit, n, place)
                    elif name == "pv":
                        pe.wait_ge(unit_free, unit - 1)
                        pe.wait_ge(pT_lo_done, h.tu + (UNITS_OF[TPC * (n + 1) - 1][-1] + 1))
                        c = PV_CHUNK[n]
                        pieces = pv_pieces(c)
                        for j, q in pieces:
                            for m, (a, b) in enumerate(three((v_hi, pT_hi), (v_lo, pT_hi), (v_hi, pT_lo))):
                                last = nc.tensor.matmul(unit_bank(place)[:, q:CH], a[:, j, :], b[c][:, j, q:CH],
                                                        start=(j == 0 and m == 0),
                                                        stop=(j == len(pieces) - 1 and m == 2))
                        last.then_inc(unit_done, 1)
                    elif name == "out":
                        if n == 0:
                            pe.wait_ge(ow_lo_done, h.h + ST // 2 + 1)
                            pe.wait_ge(hid_lo_done, h.pair + NPAIR)
                        out_unit(unit, n, place, [(0, head_hi, head_lo)] +
                                 [(1 + b, hid_hi[:, HID_BUF[t], :], hid_lo[:, HID_BUF[t], :])
                                  for b, t in enumerate(OUT_TILES[h.hh])])

            rounds(pe, body)


def _constants(np):
    f32 = np.float32
    t = np.arange(T, dtype=f32)
    theta = np.power(f32(10000.0), (f32(-2.0) * np.arange(HALF0, dtype=f32) / f32(DH0)).astype(f32)).astype(f32)
    ang = (t[:, None] * theta[None, :]).astype(f32)
    c0, s0 = (np.tile(f(ang.astype(np.float64)).astype(f32).T, (H0, 1)) for f in (np.cos, np.sin))
    half = DS // 2
    inv = (f32(1.0) / np.power(f32(10000.0), (np.arange(half, dtype=f32) / f32(half)).astype(f32)).astype(f32)).astype(f32)
    ang1 = (t[:, None] * inv[None, :]).astype(f32)
    c1, s1 = (f(ang1.astype(np.float64)).astype(f32).T for f in (np.cos, np.sin))
    one = np.ones((DS, T), f32)
    scale0 = f32(DH0 ** -0.5)
    mask = np.where(np.arange(P)[None, :] > np.arange(P)[:, None], f32(-1e30), f32(0.0)).astype(f32)
    return {
        "ident": np.eye(P, dtype=f32), "mask": mask,
        "cos_q": c0 * scale0, "sin_q": s0 * scale0, "cos_k": c0, "sin_k": s0,
        "cos1": np.concatenate([one, c1, c1]), "sin1": np.concatenate([one, s1, -s1]),
        "iota": np.tile(np.arange(NE, dtype=f32), (P, 1)),
    }


def _layout(np, a):
    def kp(w):
        return w.reshape(KT, P, -1).transpose(1, 0, 2)

    def rows(w):
        return w.reshape(-1, P, w.shape[-1]).transpose(1, 0, 2)

    even = [h * DH0 + 2 * i for h in range(H0) for i in range(HALF0)]
    odd = [n + 1 for n in even]
    wq, wk, wv = a["L0_attn_Wq"], a["L0_attn_Wk"], a["L0_attn_Wv"]
    out = {"x": a["L0_attn_X"][0]}
    out["w_qkv0"] = kp(np.concatenate([wq[even].T, wq[odd].T, wk[even].T, wk[odd].T, wv.T], axis=1))
    out["up0"] = kp(a["L0_ffn_up_weight"].T)
    out["down0"] = rows(a["L0_ffn_down_weight"].T)
    out["up_scale"] = a["L0_ffn_up_scale"].reshape(UT, P).T
    out["down_scale"] = np.tile(a["L0_ffn_down_scale"], (P, 1))
    out["out_scale"] = np.tile(a["L0_ffn_output_scale"], (P, 1))
    wo = np.zeros((H0, 2 * DH0, D), np.float32)
    wo[:, :DH0] = a["L0_attn_Wo"].T.reshape(H0, DH0, D)
    out["wo0"] = rows(wo.reshape(-1, D))
    pad = np.zeros((D, 1), np.float32)
    out["router"] = kp(np.concatenate([a["L1_ffn_gate_w"].T, a["L1_ffn_shared_expert_gate_w"].T, pad], axis=1))
    parts = []
    for h in range(H1):
        s = slice(h * DS, (h + 1) * DS)
        w = np.concatenate([a["L1_attn_wq_sem"][:, s], a["L1_attn_wq_geo"][:, s], a["L1_attn_wk_sem"][:, s],
                            a["L1_attn_wk_geo"][:, s], a["L1_attn_wv"][:, h * DV:(h + 1) * DV]], axis=1)
        parts.append(kp(w).reshape(P, -1))
    out["w_qkv1"] = np.stack(parts)
    out["gate_logit"] = np.tile(a["L1_attn_gate_logit"], (P, 1))
    rw = P // EG
    gu = a["L1_ffn_gate_up_proj"].reshape(NEG, EG, 2, ET, rw, KT, P)
    out["gu1"] = gu.transpose(0, 3, 6, 5, 2, 1, 4).reshape(NEG * ET, P, -1)
    dn = a["L1_ffn_down_proj"].reshape(NEG, EG, D, ET, rw).transpose(0, 3, 1, 4, 2).reshape(NEG, ET, P, D)
    wo1 = a["L1_attn_wo"].reshape(NEG, HPI, DV, D)
    out["ow_a"] = np.stack([wo1[:, 0], dn[:, 0]], axis=2)
    out["ow_b"] = np.stack([wo1[:, 1], dn[:, 1], dn[:, 2]], axis=2)
    sg = np.stack([a["L1_ffn_shared_gate_w"], a["L1_ffn_shared_up_w"]])
    out["gu_shared"] = sg.reshape(2, ST, P, KT, P).transpose(1, 4, 3, 0, 2).reshape(ST, P, -1)
    out["down_shared"] = a["L1_ffn_shared_down_w"].T.reshape(ST // 2, 2, P, D).transpose(0, 2, 1, 3)
    return out


def kernel(**inputs):
    import numpy as _np
    import concourse.bacc as _bacc
    from concourse import mybir as _mybir
    from concourse.bass_utils import run_bass_kernel_spmd as _run

    nc = _bacc.Bacc("TRN2", target_bir_lowering=False, num_devices=1)
    host = _layout(_np, {k: _np.asarray(v) for k, v in inputs.items()})
    host.update(_constants(_np))
    arrays, tensors = {}, {}
    for name, value in host.items():
        value = _np.ascontiguousarray(value)
        arrays[f"in_{name}"] = value
        tensors[name] = nc.dram_tensor(f"in_{name}", value.shape, _mybir.dt.from_np(value.dtype),
                                       kind="ExternalInput").ap()
    tensors["out"] = nc.dram_tensor("outT", (KT, P, T), _mybir.dt.float32, kind="ExternalOutput").ap()
    build(nc, tensors)
    r = _run(nc, [arrays], core_ids=[0])
    return r.results[0]["outT"].reshape(D, T).T.reshape(1, T, D)
```
